# Optimizing a Trainium2 kernel written in Bass

```python
import numpy as np
import jax
import jax.numpy as jnp

def _softmax(x, axis=-1):
    return jax.nn.softmax(x, axis=axis)

def _gelu(x):
    return jax.nn.gelu(x, approximate=True)

def _silu(x):
    return jax.nn.silu(x)

def _sigmoid(x):
    return jax.nn.sigmoid(x)

def _layernorm(x, axis=-1, eps=1e-05):
    m = jnp.mean(x, axis=axis, keepdims=True)
    v = jnp.var(x, axis=axis, keepdims=True)
    return (x - m) / jnp.sqrt(v + eps)

def _scatter_add(tgt, idx, src, axis=0):
    return tgt.at[idx].add(src)

def _segment_sum(src, seg, n):
    return jax.ops.segment_sum(src, seg, n)
kernel_name = 'mk_conv_preact_d2_conv_nchw256_r4_c495ac'

def setup_inputs(seed: int=0):
    np.random.seed(seed)
    _w = jnp.asarray

    def _rec_inputs():
        import jax
        import jax.numpy as jnp
        _gk = jax.random.key(seed)
        x = -8.268e-05 + 0.9999 * jax.random.normal(jax.random.fold_in(_gk, 1), (16, 64, 56, 56), jnp.float32)
        return x
    x = _rec_inputs()

    def _L0_conv_setup():
        import jax, jax.numpy as jnp
        import numpy as np
        EPS = 0.0001

        def _zca_forward(x, weight, bias, groups=16):
            N, C, H, W = x.shape
            G = groups
            c = C // G
            M = N * H * W
            xf = jnp.transpose(x, (1, 0, 2, 3)).reshape(C, M)
            mu = jnp.mean(xf, axis=1, keepdims=True)
            xc = xf - mu
            xg = xc.reshape(G, c, M)
            cov = jnp.einsum('gim,gjm->gij', xg, xg) / M
            cov = cov + EPS * jnp.eye(c, dtype=x.dtype)
            e, v = jnp.linalg.eigh(cov)
            inv_sqrt = jax.lax.rsqrt(e)
            proj = jnp.einsum('gik,gk,gjk->gij', v, inv_sqrt, v)
            xw = jnp.einsum('gij,gjm->gim', proj, xg).reshape(C, M)
            out = xw * weight + bias
            return jnp.transpose(out.reshape(C, N, H, W), (1, 0, 2, 3))
        key = jax.random.key(seed)
        k1, k2 = jax.random.split(key)
        N, C, H, W = (16, 64, 56, 56)
        x = jax.random.normal(k1, (N, C, H, W), dtype=jnp.float32)
        weight = jax.random.uniform(k2, (C, 1), dtype=jnp.float32)
        bias = jnp.zeros((C, 1), dtype=jnp.float32)
        return {'x': x, 'weight': weight, 'bias': bias}
    _L0_conv_all = _L0_conv_setup()
    _L0_conv_in = {k: v for k, v in _L0_conv_all.items() if k in ('weight', 'bias')}
    del _L0_conv_all

    def _L1_conv_setup():
        import jax, jax.numpy as jnp
        import numpy as np
        B, C, H, W = (16, 64, 56, 56)
        HEADS, DH, WS = (16, 16, 7)
        EPS = 1e-06
        key = jax.random.key(seed)
        k1, k2, k3 = jax.random.split(key, 3)
        return {'x': jax.random.normal(k1, (B, C, H, W), jnp.float32), 'bn_gamma': jnp.ones((C,), jnp.float32), 'bn_beta': jnp.zeros((C,), jnp.float32), 'bn_mean': jnp.zeros((C,), jnp.float32), 'bn_var': jnp.ones((C,), jnp.float32), 'qk_w': jax.random.normal(k2, (2 * C, C), jnp.float32) * 0.02, 'v_w': jax.random.normal(k3, (C, C), jnp.float32) * 0.02}
    _L1_conv_all = _L1_conv_setup()
    _L1_conv_in = {k: v for k, v in _L1_conv_all.items() if k in ('bn_gamma', 'bn_beta', 'bn_mean', 'bn_var', 'qk_w', 'v_w')}
    del _L1_conv_all
    return {'x': x, 'L0_conv_weight': _L0_conv_in['weight'], 'L0_conv_bias': _L0_conv_in['bias'], 'L1_conv_bn_gamma': _L1_conv_in['bn_gamma'], 'L1_conv_bn_beta': _L1_conv_in['bn_beta'], 'L1_conv_bn_mean': _L1_conv_in['bn_mean'], 'L1_conv_bn_var': _L1_conv_in['bn_var'], 'L1_conv_qk_w': _L1_conv_in['qk_w'], 'L1_conv_v_w': _L1_conv_in['v_w']}

def reference(x, L0_conv_weight, L0_conv_bias, L1_conv_bn_gamma, L1_conv_bn_beta, L1_conv_bn_mean, L1_conv_bn_var, L1_conv_qk_w, L1_conv_v_w):
    import jax
    import jax.numpy as jnp

    def _L0_conv_ref(x, weight, bias):
        import jax, jax.numpy as jnp
        import numpy as np
        EPS = 0.0001

        def _zca_forward(x, weight, bias, groups=16):
            N, C, H, W = x.shape
            G = groups
            c = C // G
            M = N * H * W
            xf = jnp.transpose(x, (1, 0, 2, 3)).reshape(C, M)
            mu = jnp.mean(xf, axis=1, keepdims=True)
            xc = xf - mu
            xg = xc.reshape(G, c, M)
            cov = jnp.einsum('gim,gjm->gij', xg, xg) / M
            cov = cov + EPS * jnp.eye(c, dtype=x.dtype)
            e, v = jnp.linalg.eigh(cov)
            inv_sqrt = jax.lax.rsqrt(e)
            proj = jnp.einsum('gik,gk,gjk->gij', v, inv_sqrt, v)
            xw = jnp.einsum('gij,gjm->gim', proj, xg).reshape(C, M)
            out = xw * weight + bias
            return jnp.transpose(out.reshape(C, N, H, W), (1, 0, 2, 3))
        return _zca_forward(x, weight, bias)

    def _L1_conv_ref(x, bn_gamma, bn_beta, bn_mean, bn_var, qk_w, v_w):
        import jax, jax.numpy as jnp
        import numpy as np
        B, C, H, W = (16, 64, 56, 56)
        HEADS, DH, WS = (16, 16, 7)
        EPS = 1e-06
        Bb, Cc, Hh, Ww = x.shape
        scale = DH ** (-0.5)
        inv = bn_gamma / jnp.sqrt(bn_var + EPS)
        xn = (x - bn_mean[:, None, None]) * inv[:, None, None] + bn_beta[:, None, None]
        n1, n2 = (Hh // WS, Ww // WS)
        t = xn.reshape(Bb, Cc, WS, n1, WS, n2).transpose(0, 3, 5, 2, 4, 1)
        tok = t.reshape(Bb * n1 * n2, WS * WS, Cc)
        qk = (tok @ qk_w.T).reshape(-1, WS * WS, 2, HEADS, DH)
        q = qk[:, :, 0].transpose(0, 2, 1, 3)
        k = qk[:, :, 1].transpose(0, 2, 1, 3)
        attn = jax.nn.softmax(jnp.einsum('bhqd,bhkd->bhqk', q, k) * scale, axis=-1)
        v = jax.nn.relu(tok @ v_w.T).reshape(-1, WS * WS, HEADS, DH).transpose(0, 2, 1, 3)
        o = jnp.einsum('bhqk,bhkd->bhqd', attn, v)
        o = o.transpose(0, 2, 1, 3).reshape(Bb, n1, n2, WS, WS, Cc)
        out = o.transpose(0, 5, 3, 1, 4, 2).reshape(Bb, Cc, Hh, Ww)
        return out

    def _gn(v, G=32, eps=1e-05):
        B_, C_, H_, W_ = v.shape
        g = v.reshape(B_, G, C_ // G, H_, W_)
        m = jnp.mean(g, axis=(2, 3, 4), keepdims=True)
        s = jnp.var(g, axis=(2, 3, 4), keepdims=True)
        return ((g - m) / jnp.sqrt(s + eps)).reshape(v.shape)

    def _ln_c(v, eps=1e-06):
        m = jnp.mean(v, axis=1, keepdims=True)
        s = jnp.var(v, axis=1, keepdims=True)
        return (v - m) / jnp.sqrt(s + eps)

    def _ln_t(v, eps=1e-05):
        m = jnp.mean(v, axis=-1, keepdims=True)
        s = jnp.var(v, axis=-1, keepdims=True)
        return (v - m) / jnp.sqrt(s + eps)

    def _to_tokens(v):
        B_, C_, H_, W_ = v.shape
        return v.reshape(B_, C_, H_ * W_).transpose(0, 2, 1)

    def _from_tokens(t, like):
        B_, C_, H_, W_ = like.shape
        return t.transpose(0, 2, 1).reshape(B_, C_, H_, W_)
    x = x + _L0_conv_ref(_gn(x), L0_conv_weight, L0_conv_bias)
    x = x + _L1_conv_ref(_gn(x), L1_conv_bn_gamma, L1_conv_bn_beta, L1_conv_bn_mean, L1_conv_bn_var, L1_conv_qk_w, L1_conv_v_w)
    return x

_drawn_inputs = setup_inputs


def setup_inputs(seed=0):
    import zlib

    import numpy as np

    out = dict(_drawn_inputs(seed))
    spreads = {'L0_conv_bias': (0.0, 0.1),
     'L1_conv_bn_gamma': (1.0, 0.6),
     'L1_conv_bn_beta': (0.0, 0.8),
     'L1_conv_bn_mean': (0.0, 0.8),
     'L1_conv_bn_var': (1.0, 0.6)}
    factors = {'L1_conv_qk_w': 8.0, 'L1_conv_v_w': 4.295}
    for name, (base, spread) in spreads.items():
        noise = np.random.default_rng([zlib.crc32(name.encode()), seed]).standard_normal(out[name].shape)
        drawn = base * np.exp(spread * noise) if base else spread * noise
        out[name] = jnp.asarray(drawn.astype(out[name].dtype))
    for name, factor in factors.items():
        out[name] = (out[name] * factor).astype(out[name].dtype)
    return out
```

```python
from contextlib import ExitStack

import numpy as np
import concourse.bass as bass
from concourse import mybir

F32 = mybir.dt.float32
BF16 = mybir.dt.bfloat16
ALU = mybir.AluOpType
ACT = mybir.ActivationFunctionType
AX = mybir.AxisListType

N, C, H, W = 16, 64, 56, 56
P = 128
PAIRS = N // 2
HW = H * W
WS, NW = 7, H // 7
POS = WS * WS
SUB = 4
TOK = POS * SUB
KH = NW // SUB
UNITS = PAIRS * NW
UT = KH * TOK
HEADS, DH = 16, 16
HH = HEADS // 2
TILES = KH * 2
ST = HH * POS
ZG = 4
SCALE = DH ** -0.5

GN_EPS, BN_EPS, ZCA_EPS = 1e-5, 1e-6, 1e-4
GN_COUNT = 2 * HW
ZCA_COUNT = N * HW

BLK = 112
CB = 4
CHUNK = BLK * CB
CHUNKS = HW // CHUNK


def newton_schulz_scales():
    top = ZG + 2 * ZCA_EPS
    low = (0.5 * ZCA_EPS / top) ** 0.5
    scales = []
    while low < 1 - 1e-3:
        a = (3.0 / (1 + low + low * low)) ** 0.5
        scales.append(a)
        low = a * low * (3 - a * a * low * low) / 2
    return top, scales + [1.0, 1.0]


def conv_preact_kernel(nc, x, params, w_qk, w_v, out):
    top, scales = newton_schulz_scales()
    NS = len(scales)
    x_d = x.rearrange("(p i) (j d) h w -> p j i d (h w)", i=2, j=4)
    out_d = out.rearrange("(p i) (j d) h w -> p j i d (h w)", i=2, j=4)
    BANDS = [(j, i) for j in range(4) for i in range(2)]

    with ExitStack() as ctx:
        def sb(name, shape, dt=F32):
            return ctx.enter_context(nc.sbuf_tensor(name, shape, dt))

        def sem(name):
            return ctx.enter_context(nc.semaphore(name))

        X = sb("X", [P, PAIRS, HW])
        prm = sb("prm", [P, 6])
        wqk = sb("wqk", [P, 2, P])
        wv = sb("wv", [P, 2, C])
        ident = sb("ident", [P, P])
        identb = sb("identb", [P, P], BF16)
        blockm = sb("blockm", [P, P])
        pairm = sb("pairm", [P, P])
        foldm = sb("foldm", [P, P])
        e4 = sb("e4", [P, ZG])
        headm = sb("headm", [64, HH])
        sel = sb("sel", [P, 8, POS], BF16)
        ones_kd = sb("ones_kd", [P, 32])

        sums = sb("sums", [P, PAIRS])
        g5 = sb("g5", [P, PAIRS, 1 + ZG])
        gmask = sb("gmask", [P, P])
        t84 = sb("t84", [P, PAIRS, ZG])
        t84b = sb("t84b", [P, PAIRS, ZG])
        c84 = sb("c84", [P, PAIRS, ZG])
        sd = sb("sd", [P, 2, PAIRS])
        mean = sb("mean", [P, PAIRS])
        var = sb("var", [P, PAIRS])
        std = sb("std", [P, PAIRS])
        rinv = sb("rinv", [P, PAIRS])
        usum = sb("usum", [P, PAIRS])
        t8 = sb("t8", [P, PAIRS])
        t8b = sb("t8b", [P, PAIRS])
        v3 = sb("v3", [P, 3, PAIRS, ZG])
        v3n = sb("v3n", [P, 3, PAIRS, ZG])
        cz = sb("cz", [P, 1 + ZG])
        cm = sb("cm", [P, 1 + ZG])
        mu4 = sb("mu4", [P, ZG])
        cov4 = sb("cov4", [P, ZG])
        Yb = sb("Yb", [P, 2, P])
        Zb = sb("Zb", [P, 2, P])
        Tm = sb("Tm", [P, P])
        diagw = sb("diagw", [P, P])
        pw = sb("pw", [P, P])
        p4w = sb("p4w", [P, ZG])
        dvec = sb("dvec", [P, PAIRS])
        a4 = sb("a4", [P, PAIRS, ZG])
        ag = sb("ag", [P, PAIRS, 1 + ZG])
        amat = sb("amat", [P, 2, P])
        bninv = sb("bninv", [P, 3])
        xn_scale = sb("xn_scale", [P, PAIRS])
        xn_bias = sb("xn_bias", [P, PAIRS])
        xstage = sb("xstage", [P, 2, CHUNK])
        xT = sb("xT", [BLK, 2, CB, P + 1])

        xn = [sb(f"xn{b}", [P, KH, TOK]) for b in range(2)]
        qk = [sb(f"qk{b}", [P, 2, KH, SUB, POS]) for b in range(2)]
        diag = [sb(f"diag{b}", [P, HH, 2, KH, SUB, POS]) for b in range(2)]
        rmax = [sb(f"rmax{b}", [P, TILES, HH], BF16) for b in range(2)]
        mdiag = [sb(f"mdiag{b}", [P, HH, POS], BF16) for b in range(2)]
        prob = [sb(f"prob{b}", [P, TILES, HH, POS]) for b in range(2)]
        vst = [sb(f"vst{b}", [P, KH, SUB, 4, 2, DH]) for b in range(2)]
        rden = sb("rden", [P, KH, SUB, POS])
        otok = [sb(f"otok{b}", [P, KH, TOK]) for b in range(2)]

        ps = ctx.enter_context(nc.psum_tensor("ps", [P, 8, 512], F32))
        B_QK, B_V, B_S, B_ST, B_O = 0, 1, (2, 3), (4, 5), (6, 7)

        names = (
            "const_dma pool_chain masks_ready dve_masks psum_zero load0 load1 staged transposed "
            "xT_ready gram_chunk gram_part gram_kept dve_chain "
            "sums_ready gmean_ps var_ready std_ready vec_ready vec4_ps cov_part cov_ps mu_ready mu4_ps "
            "ns_in ns_m ns_t ns_y_ps ns_z_ps ns_y ns_z diagw_ready pw_ps pw_ready dv_ps d_ready "
            "amat_ready mix_ps mix_act mix_dve ag_ps sums2_ready gmean2_ps var2_ready std2_ready "
            "xn_ready qk_ps qk_ready diag0 diag1 v_ps v_act v_dve "
            "s_ps max_ready mt_ps mdiag_ready st_ps prob_ready pv_ps rden_ready o_ready x_ready stored"
        ).split()
        S = {n: sem(n) for n in names}
        load = [S["load0"], S["load1"]]
        diag_in = [S["diag0"], S["diag1"]]
        block = ctx.enter_context(nc.Block())

        def after(eng, name, count):
            if isinstance(count, int) and count <= 0:
                return
            eng.wait_ge(S[name], count)

        def pipeline(eng, body):
            for i in range(-2, 4):
                body(i, i % 2)
            with eng.Fori(0, UNITS // 2 - 3) as q:
                body(2 * q + 4, 0)
                body(2 * q + 5, 1)
            for i in range(UNITS - 2, UNITS + 1):
                body(i, i % 2)

        def has(u):
            return not isinstance(u, int) or 0 <= u < UNITS

        @block.sync
        def _(sp):
            for t, src in ((prm[:], params), (wqk[:], w_qk), (wv[:], w_v)):
                sp.dma_start(t, src).then_inc(S["const_dma"], 16)

            def load_pair(p, b):
                for n, (j, i) in enumerate(BANDS):
                    sp.dma_start(X[16 * n:16 * n + 16, p, :], x_d[p, j, i]).then_inc(load[b], 16)
            for b in range(2):
                load_pair(b, b)
            with sp.Fori(1, PAIRS // 2) as q:
                for b in range(2):
                    sp.wait_ge(load[b], 16 * len(BANDS) * q)
                    load_pair(2 * q + b, b)

            def spread(u, par):
                free, ready = sp.snap(TILES * (u - 1)) if not isinstance(u, int) else TILES * (u - 1), 2 * (u + 1)
                after(sp, "st_ps", free)
                after(sp, "qk_ready", ready)
                for h in range(HH):
                    r = slice(16 * h, 16 * h + 16)
                    sp.dma_start(diag[par][r, h].rearrange("p i k a s -> p (i k a s)"),
                                 qk[par][r].rearrange("p i k a s -> p (i k a s)")).then_inc(diag_in[par], 16)

            def store(p, bands):
                for n in bands:
                    sp.dma_start(out_d[p, BANDS[n][0], BANDS[n][1]], X[16 * n:16 * n + 16, p, :]
                                 ).then_inc(S["stored"], 16)

            sp.wait_ge(S["masks_ready"], 1)
            for i in range(NW):
                spread(i, i % 2)
            with sp.Fori(1, PAIRS) as p:
                for i in range(NW):
                    spread(p * NW + i, i % 2)
                    if 3 <= i < 7:
                        sp.wait_ge(S["x_ready"], KH * NW * p)
                        store(p - 1, (2 * (i - 3), 2 * (i - 3) + 1))
            sp.wait_ge(S["x_ready"], KH * UNITS)
            store(PAIRS - 1, range(len(BANDS)))
            sp.wait_ge(S["stored"], 16 * len(BANDS) * PAIRS)

        @block.gpsimd
        def _(pool):
            steps = [0]

            def chain(ins):
                steps[0] += 1
                ins.then_inc(S["pool_chain"], 1)
                pool.wait_ge(S["pool_chain"], steps[0])

            g = nc.gpsimd
            chain(g.memset(ident[:], 0.0))
            chain(g.affine_select(out=ident[:], in_=ident[:], compare_op=ALU.not_equal, fill=1.0, base=0,
                                  pattern=[[-1, P]], channel_multiplier=1))
            for m, k, value in ((blockm, ZG, 1.0), (pairm, 2, 1.0 / GN_COUNT)):
                chain(g.memset(m[:], value))
                v = m[:].rearrange("p (b e) -> p b e", e=k)
                chain(g.affine_select(out=v, in_=v, compare_op=ALU.is_ge, fill=0.0, base=0,
                                      pattern=[[-k, P // k], [0, k]], channel_multiplier=1))
                chain(g.affine_select(out=v, in_=v, compare_op=ALU.is_ge, fill=0.0, base=k - 1,
                                      pattern=[[k, P // k], [0, k]], channel_multiplier=-1))
            chain(g.memset(ones_kd[:], 0.0))
            chain(g.memset(ones_kd[0:POS, 0:16], 1.0))
            chain(g.memset(ones_kd[64:64 + POS, 16:32], 1.0))
            for b in range(2):
                chain(g.memset(vst[b][:], 0.0))
                chain(g.memset(diag[b][:], 0.0))
                chain(g.memset(mdiag[b][:], 0.0))
            g.memset(xT[:, :, :, P:P + 1], 1.0).then_inc(S["masks_ready"], 1)

            def body(i, par):
                v = i - 1
                if has(v):
                    after(pool, "o_ready", KH * (v + 1))
                    xv = X[:, v // NW, :].rearrange("p (a i c k w) -> p i k a c w", a=WS, i=NW, c=WS, k=KH)
                    for k in range(KH):
                        xp = xv[:, v % NW, k].rearrange("p a c w -> p w a c")
                        g.tensor_tensor(xp, xp, otok[1 - par][:, k, :].rearrange("p (w a c) -> p w a c", w=SUB, a=WS),
                                        ALU.add).then_inc(S["x_ready"], 1)
            pipeline(pool, body)

        @block.scalar
        def _(act):
            a = nc.scalar

            def gram_evacuate(p, c, b):
                n = p * CHUNKS + c
                act.wait_ge(S["transposed"], n + 1)
                after(act, "gram_chunk", n - 1)
                a.activation(xT[:, b, :, 0:P], ps[0:BLK, b, 0:CB * P].rearrange("q (k c) -> q k c", k=CB),
                             ACT.Copy).then_inc(S["xT_ready"], 1)

            act.wait_ge(S["masks_ready"], 1)
            for c in range(CHUNKS):
                gram_evacuate(0, c, c % 2)
            with act.Fori(0, PAIRS // 2 - 1) as q:
                p = 2 * q + 1
                for b in range(2):
                    for c in range(CHUNKS):
                        gram_evacuate(p + b, c, (1 + b + c) % 2)
            for c in range(CHUNKS):
                gram_evacuate(PAIRS - 1, c, (PAIRS - 1 + c) % 2)

            act.wait_ge(S["var_ready"], 1)
            a.activation(std[:], var[:], ACT.Sqrt).then_inc(S["std_ready"], 1)
            for n in range(NS):
                act.wait_ge(S["ns_y_ps"], n + 1)
                a.activation(Yb[:, (n + 1) % 2, :], ps[:, 1, 0:P], ACT.Copy).then_inc(S["ns_y"], 1)

            def mix(p, c, b):
                n = p * NW + c
                act.wait_ge(S["mix_ps"], n + 1)
                a.activation(X[:, p, c * 392:(c + 1) * 392], ps[:, 2 + c % 4, 0:392], ACT.Identity,
                             bias=dvec[:, bass.ds(p, 1)]).then_inc(S["mix_act"], 1)
            act.wait_ge(S["d_ready"], 1)
            with act.Fori(0, PAIRS) as p:
                for c in range(0, NW, 2):
                    mix(p, c, 0)

            act.wait_ge(S["var2_ready"], 1)
            a.activation(std[:], var[:], ACT.Sqrt).then_inc(S["std2_ready"], 1)
            act.wait_ge(S["var2_ready"], 2)
            a.activation(bninv[:, 1:2], bninv[:, 0:1], ACT.Sqrt).then_inc(S["std2_ready"], 1)

            def body(i, par):
                u = i
                if has(u):
                    for t in range(TILES):
                        after(act, "st_ps", TILES * u + t + 1)
                        after(act, "pv_ps", TILES * (u - 2) + t + 1)
                        a.activation(prob[par][:, t], ps[:, B_ST[t % 2], 0:ST].rearrange("p (h q) -> p h q", h=HH),
                                     ACT.Exp, scale=SCALE).then_inc(S["prob_ready"], 1)
                v = i + 1
                if has(v):
                    after(act, "v_ps", v + 1)
                    after(act, "pv_ps", TILES * (v - 1))
                    a.activation(vst[1 - par][0:POS, :, :, :, 0, :],
                                 ps[0:POS, B_V, :].rearrange("p (k s j d) -> p k s j d", k=KH, s=SUB, j=4),
                                 ACT.Relu).then_inc(S["v_act"], 1)
                w = i + 2
                if has(w):
                    for m in range(2):
                        after(act, "qk_ps", 2 * w + m + 1)
                        after(act, "st_ps", TILES * (w - 1))
                        a.activation(qk[par][:, m],
                                     ps[:, B_QK, 0:UT].rearrange("p (k s a) -> p k a s", k=KH, a=SUB),
                                     ACT.Copy).then_inc(S["qk_ready"], 1)
            pipeline(act, body)

        @block.vector
        def _(dve):
            v = nc.vector
            steps = [0]

            def chain(ins):
                steps[0] += 1
                ins.then_inc(S["dve_chain"], 1)
                dve.wait_ge(S["dve_chain"], steps[0])

            v.memset(ps[:], 0.0).then_inc(S["psum_zero"], 1)
            dve.wait_ge(S["masks_ready"], 1)
            v.tensor_copy(identb[:], ident[:])
            v.tensor_reduce(e4[:], ident[:].rearrange("p (b e) -> p e b", e=ZG), AX.X, ALU.add)
            v.tensor_reduce(headm[:], ident[0:64, 0:64].rearrange("p (b e) -> p e b", e=HH), AX.X, ALU.add, negate=True)
            chain(v.tensor_reduce(t8[:], ident[:, 0:64].rearrange("p (g e) -> p g e", e=8), AX.X, ALU.add))
            v.tensor_copy(sel[:], t8[:].rearrange("p (g o) -> p g o", o=1).broadcast_to([P, 8, POS]))
            iv = ident[:].rearrange("p (j i d) -> p j i d", j=4, i=2)
            fv = foldm[:].rearrange("p (j i d) -> p j i d", j=4, i=2)
            v.tensor_tensor(fv[:, :, 0, :], iv[:, :, 0, :], iv[:, :, 1, :], ALU.add)
            chain(v.tensor_tensor(fv[:, :, 1, :], iv[:, :, 0, :], iv[:, :, 1, :], ALU.add))
            chain(v.tensor_scalar(foldm[:], foldm[:], 1.0 / ZCA_COUNT, None, ALU.mult))
            v.memset(bninv[:], 0.0).then_inc(S["dve_masks"], 1)
            dve.wait_ge(S["dve_masks"], 1)

            def stage(p, c, b):
                n = p * CHUNKS + c
                after(dve, "transposed", n - 1)
                v.tensor_copy(xstage[:, b, :], X[:, p, c * CHUNK:(c + 1) * CHUNK]).then_inc(S["staged"], 1)

            def keep_gram(p, b):
                dve.wait_ge(S["gram_chunk"], CHUNKS * (p + 1))
                after(dve, "gram_kept", p)
                v.tensor_tensor(gmask[:], ps[:, 2 + b, 0:P], blockm[:], ALU.mult).then_inc(S["gram_part"], 1)
                v.tensor_copy(g5[:, bass.ds(p, 1), 0:1], ps[:, 2 + b, P:P + 1].rearrange("p (a b) -> p a b", a=1)
                              ).then_inc(S["gram_part"], 1)
                dve.wait_ge(S["gram_part"], 2 * (p + 1))
                v.tensor_reduce(g5[:, bass.ds(p, 1), 1:], gmask[:].rearrange("p (o b e) -> p o e b", o=1, e=ZG),
                                AX.X, ALU.add).then_inc(S["gram_kept"], 1)

            def stage_pair(p, b, first=False):
                dve.wait_ge(load[b], 16 * 8 * (p // 2 + 1))
                for c in range(CHUNKS):
                    stage(p, c, (b + c) % 2)
                    if c == 2 and not first:
                        keep_gram(p - 1, 1 - b)
            stage_pair(0, 0, first=True)
            stage_pair(1, 1)
            stage_pair(2, 0)
            with dve.Fori(1, PAIRS // 2 - 1) as q:
                stage_pair(2 * q + 1, 1)
                stage_pair(2 * q + 2, 0)
            stage_pair(PAIRS - 1, 1)
            keep_gram(PAIRS - 1, 1)
            dve.wait_ge(S["gram_kept"], PAIRS)

            def over_pairs(ap):
                return ap.rearrange("p (n o) -> p n o", o=1).broadcast_to([P, PAIRS, ZG])

            def over_group(ap):
                return ap.rearrange("p (o e) -> p o e", o=1).broadcast_to([P, PAIRS, ZG])

            def rsqrt(y, x_, s_, t_):
                chain(v.reciprocal(y, s_))
                chain(v.tensor_tensor(t_, y, y, ALU.mult))
                chain(v.tensor_tensor(t_, t_, x_, ALU.mult))
                chain(v.tensor_scalar(t_, t_, -0.5, 1.5, ALU.mult, ALU.add))
                chain(v.tensor_tensor(y, y, t_, ALU.mult))

            chain(v.tensor_tensor(t84[:], g5[:, :, 1:], over_group(e4[:]), ALU.mult))
            v.tensor_copy(sd[:, 0, :], g5[:, :, 0])
            v.tensor_copy(sums[:], g5[:, :, 0])
            chain(v.tensor_reduce(sd[:, 1, :], t84[:], AX.X, ALU.add))
            v.tensor_copy(t8b[:], sums[:]).then_inc(S["sums_ready"], 1)
            dve.wait_ge(S["gmean_ps"], 1)

            def group_var(col):
                chain(v.tensor_copy(mean[:], ps[:, 0, col:col + PAIRS]))
                chain(v.tensor_tensor(t8[:], mean[:], mean[:], ALU.mult))
                return v.scalar_tensor_tensor(var[:], ps[:, 0, col + PAIRS:col + 2 * PAIRS], GN_EPS, t8[:],
                                              ALU.add, ALU.subtract)
            dve.wait_ge(S["sums_ready"], 1)
            group_var(0).then_inc(S["var_ready"], 1)
            dve.wait_ge(S["var_ready"], 1)
            dve.wait_ge(S["std_ready"], 1)
            rsqrt(rinv[:], var[:], std[:], t8[:])
            chain(v.scalar_tensor_tensor(usum[:], mean[:], -float(HW), sums[:], ALU.mult, ALU.add))
            for k, vec in enumerate((rinv, mean, sums)):
                v.tensor_tensor(v3[:, k], over_pairs(vec[:]), over_group(e4[:]), ALU.mult).then_inc(S["vec_ready"], 1)
            dve.wait_ge(S["vec4_ps"], 1)
            chain(v.tensor_copy(v3n[:], ps[:, 1, 0:3 * PAIRS * ZG].rearrange("p (k n e) -> p k n e", k=3, n=PAIRS)))
            chain(v.tensor_tensor(t84[:], v3n[:, 1], over_pairs(usum[:]), ALU.mult))
            chain(v.tensor_tensor(t84b[:], v3n[:, 2], over_pairs(mean[:]), ALU.mult))
            chain(v.tensor_tensor(c84[:], g5[:, :, 1:], t84[:], ALU.subtract))
            chain(v.tensor_tensor(c84[:], c84[:], t84b[:], ALU.subtract))
            chain(v.tensor_tensor(c84[:], c84[:], v3n[:, 0], ALU.mult))
            chain(v.tensor_tensor(c84[:], c84[:], over_pairs(rinv[:]), ALU.mult))
            chain(v.tensor_tensor(t8[:], usum[:], rinv[:], ALU.mult))
            v.tensor_reduce(cz[:, 0:1], t8[:], AX.X, ALU.add).then_inc(S["cov_part"], 1)
            v.tensor_reduce(cz[:, 1:], c84[:].rearrange("p n e -> p e n"), AX.X, ALU.add).then_inc(S["cov_part"], 1)
            dve.wait_ge(S["cov_ps"], 1)
            chain(v.tensor_copy(cm[:], ps[:, 2, 0:1 + ZG]))
            v.tensor_scalar(mu4[:], e4[:], cm[:, 0:1], None, ALU.mult).then_inc(S["mu_ready"], 1)
            dve.wait_ge(S["mu4_ps"], 1)
            chain(v.tensor_scalar(cov4[:], ps[:, 3, 0:ZG], cm[:, 0:1], None, ALU.mult))
            chain(v.tensor_tensor(cov4[:], cm[:, 1:], cov4[:], ALU.subtract))
            chain(v.scalar_tensor_tensor(cov4[:], e4[:], ZCA_EPS, cov4[:], ALU.mult, ALU.add))
            chain(v.tensor_scalar(cov4[:], cov4[:], 1.0 / top, None, ALU.mult))
            v.tensor_copy(Zb[:, 0, :], ident[:]).then_inc(S["ns_in"], 1)
            v.tensor_tensor(Yb[:, 0, :].rearrange("p (b e) -> p b e", e=ZG), blockm[:].rearrange("p (b e) -> p b e", e=ZG),
                            cov4[:].rearrange("p (o e) -> p o e", o=1).broadcast_to([P, P // ZG, ZG]), ALU.mult
                            ).then_inc(S["ns_in"], 1)
            for n, s in enumerate(scales):
                dve.wait_ge(S["ns_m"], n + 1)
                chain(v.tensor_scalar(Tm[:], ident[:], 1.5 * s, None, ALU.mult))
                v.scalar_tensor_tensor(Tm[:], ps[:, 0, 0:P], -0.5 * s ** 3, Tm[:], ALU.mult, ALU.add
                                       ).then_inc(S["ns_t"], 1)
                dve.wait_ge(S["ns_z_ps"], n + 1)
                v.tensor_copy(Zb[:, (n + 1) % 2, :], ps[:, 2, 0:P]).then_inc(S["ns_z"], 1)
            Zn = Zb[:, NS % 2, :]
            dve.wait_ge(S["const_dma"], 48)
            v.tensor_scalar(diagw[:], ident[:], prm[:, 0:1], top ** -0.5, ALU.mult, ALU.mult).then_inc(S["diagw_ready"], 1)
            dve.wait_ge(S["ns_z"], NS)
            chain(v.tensor_reduce(p4w[:], Zn.rearrange("p (b e) -> p e b", e=ZG), AX.X, ALU.add))
            chain(v.tensor_scalar(p4w[:], p4w[:], prm[:, 0:1], top ** -0.5, ALU.mult, ALU.mult))
            chain(v.tensor_tensor(t8[:], rinv[:], mean[:], ALU.mult))
            chain(v.tensor_scalar(t8[:], t8[:], cm[:, 0:1], None, ALU.add))
            chain(v.tensor_tensor(a4[:], v3n[:, 0], p4w[:].rearrange("p (o e) -> p o e", o=1).broadcast_to([P, PAIRS, ZG]), ALU.mult))
            chain(v.tensor_tensor(a4[:], a4[:], over_group(e4[:]), ALU.add))
            dve.wait_ge(S["pw_ps"], 1)
            v.tensor_copy(pw[:], ps[:, 3, 0:P]).then_inc(S["pw_ready"], 1)
            dve.wait_ge(S["dv_ps"], 1)
            v.tensor_scalar(dvec[:], ps[:, 4, 0:PAIRS], -1.0, prm[:, 1:2], ALU.mult, ALU.add).then_inc(S["d_ready"], 1)
            dve.wait_ge(S["d_ready"], 1)
            dve.wait_ge(S["pw_ready"], 1)

            def mix(p, b):
                after(dve, "mix_ps", NW * (p - 1))
                v.scalar_tensor_tensor(amat[:, b, :], pw[:], rinv[:, bass.ds(p, 1)], ident[:], ALU.mult, ALU.add
                                       ).then_inc(S["amat_ready"], 1)
                for c in range(1, NW, 2):
                    dve.wait_ge(S["mix_ps"], p * NW + c + 1)
                    v.tensor_scalar(X[:, p, c * 392:(c + 1) * 392], ps[:, 2 + c % 4, 0:392],
                                    dvec[:, bass.ds(p, 1)], None, ALU.add).then_inc(S["mix_dve"], 1)
            for p in range(3):
                mix(p, p % 2)
            with dve.Fori(1, PAIRS // 2 - 1) as q:
                mix(2 * q + 1, 1)
                mix(2 * q + 2, 0)
            mix(PAIRS - 1, 1)

            dve.wait_ge(S["ag_ps"], PAIRS)
            chain(v.tensor_copy(ag[:], ps[:, 1, 0:PAIRS * (1 + ZG)].rearrange("p (n e) -> p n e", n=PAIRS)))
            chain(v.tensor_tensor(t84[:], ag[:, :, 1:], a4[:], ALU.mult))
            chain(v.tensor_reduce(t8[:], t84[:], AX.X, ALU.add))
            chain(v.scalar_tensor_tensor(sd[:, 0, :], dvec[:], float(HW), ag[:, :, 0], ALU.mult, ALU.add))
            chain(v.tensor_tensor(t8b[:], sd[:, 0, :], ag[:, :, 0], ALU.add))
            chain(v.tensor_tensor(t8b[:], t8b[:], dvec[:], ALU.mult))
            v.tensor_tensor(sd[:, 1, :], t8[:], t8b[:], ALU.add).then_inc(S["sums2_ready"], 1)
            dve.wait_ge(S["gmean2_ps"], 1)
            dve.wait_ge(S["sums2_ready"], 1)
            group_var(0).then_inc(S["var2_ready"], 1)
            v.tensor_scalar(bninv[:, 0:1], prm[:, 5:6], BN_EPS, None, ALU.add).then_inc(S["var2_ready"], 1)
            dve.wait_ge(S["var2_ready"], 2)
            dve.wait_ge(S["std2_ready"], 2)
            rsqrt(rinv[:], var[:], std[:], t8[:])
            rsqrt(bninv[:, 2:3], bninv[:, 0:1], bninv[:, 1:2], t8[:, 0:1])
            chain(v.tensor_tensor(bninv[:, 2:3], bninv[:, 2:3], prm[:, 2:3], ALU.mult))
            chain(v.tensor_scalar(xn_scale[:], rinv[:], bninv[:, 2:3], None, ALU.mult))
            chain(v.tensor_tensor(t8[:], mean[:], rinv[:], ALU.mult))
            chain(v.tensor_scalar(t8[:], t8[:], prm[:, 4:5], bninv[:, 2:3], ALU.add, ALU.mult))
            chain(v.tensor_scalar(xn_bias[:], t8[:], -1.0, prm[:, 3:4], ALU.mult, ALU.add))
            dve.wait_ge(S["mix_act"], PAIRS * NW // 2)
            dve.wait_ge(S["mix_dve"], PAIRS * NW // 2)
            v.memset(ps[:], 0.0).then_inc(S["psum_zero"], 1)
            dve.wait_ge(S["psum_zero"], 2)

            def body(i, par):
                u = i + 2
                if has(u):
                    after(dve, "v_ps", u - 1)
                    xv = X[:, u // NW, :].rearrange("p (a i c k w) -> p i k a c w", a=WS, i=NW, c=WS, k=KH)
                    for k in range(KH):
                        v.tensor_scalar(xn[par][:, k, :].rearrange("p (w a c) -> p w a c", w=SUB, a=WS),
                                        xv[:, u % NW, k].rearrange("p a c w -> p w a c"),
                                        xn_scale[:, bass.ds(u // NW, 1)], xn_bias[:, bass.ds(u // NW, 1)],
                                        ALU.mult, ALU.add).then_inc(S["xn_ready"], 1)
                w, z = i + 1, i - 1

                def divide(k):
                    after(dve, "pv_ps", TILES * z + 2 * k + 2)
                    v.reciprocal(rden[:, k].rearrange("p a s -> p (a s)"), ps[:, B_O[k], TOK:2 * TOK]
                                 ).then_inc(S["rden_ready"], 1)
                    dve.wait_ge(S["rden_ready"], KH * z + k + 1)
                    after(dve, "x_ready", KH * (z - 1))
                    v.tensor_tensor(otok[1 - par][:, k].rearrange("p (s a) -> p a s", a=SUB),
                                    ps[:, B_O[k], 0:TOK].rearrange("p (a s) -> p a s", a=SUB),
                                    rden[:, k], ALU.mult).then_inc(S["o_ready"], 1)
                if has(z):
                    divide(0)
                if has(w):
                    after(dve, "v_ps", w + 1)
                    after(dve, "pv_ps", TILES * (w - 1))
                    v.tensor_scalar(vst[1 - par][64:64 + POS, :, :, :, 1, :].rearrange("p k s j d -> p (k s j) d"),
                                    ps[64:64 + POS, B_V, :].rearrange("p (n d) -> p n d", d=DH),
                                    0.0, None, ALU.max).then_inc(S["v_dve"], 1)
                if has(z):
                    divide(1)
                if has(w):
                    for t in range(TILES):
                        after(dve, "s_ps", TILES * w + t + 1)
                        after(dve, "mt_ps", w - 1)
                        v.tensor_reduce(rmax[1 - par][:, t, :], ps[:, B_S[t % 2], 0:ST].rearrange("p (h k) -> p h k", h=HH),
                                        AX.X, ALU.max).then_inc(S["max_ready"], 1)
                    after(dve, "mt_ps", w + 1)
                    after(dve, "st_ps", TILES * (w - 1))
                    v.tensor_tensor(mdiag[1 - par][0:64],
                                    ps[0:64, B_S[0], 448:448 + POS].rearrange("p (o q) -> p o q", o=1).broadcast_to([64, HH, POS]),
                                    headm[:].rearrange("p (h o) -> p h o", o=1).broadcast_to([64, HH, POS]),
                                    ALU.mult).then_inc(S["mdiag_ready"], 1)
            pipeline(dve, body)

        @block.tensor
        def _(pe):
            mm = nc.tensor.matmul

            def transposes(p, c, b):
                n = p * CHUNKS + c
                pe.wait_ge(S["staged"], n + 1)
                after(pe, "xT_ready", n - 1)
                for k in range(CB):
                    ins = nc.tensor.transpose(ps[0:BLK, b, k * P:(k + 1) * P], xstage[:, b, k * BLK:(k + 1) * BLK], ident[:])
                ins.then_inc(S["transposed"], 1)

            def gram(p, c, b, pb):
                pe.wait_ge(S["xT_ready"], p * CHUNKS + c + 1)
                if c == 0:
                    after(pe, "gram_kept", p - 1)
                for k in range(CB):
                    ins = mm(ps[:, 2 + pb, 0:P + 1], xT[:, b, k, 0:P], xT[:, b, k, :],
                             start=(c == 0 and k == 0), stop=(c == CHUNKS - 1 and k == CB - 1))
                ins.then_inc(S["gram_chunk"], 1)

            def gram_steps(p, pb, first=False):
                for c in range(CHUNKS):
                    b = (pb + c) % 2
                    transposes(p, c, b)
                    if c > 0:
                        gram(p, c - 1, 1 - b, pb)
                    elif not first:
                        gram(p - 1, CHUNKS - 1, 1 - b, 1 - pb)
            pe.wait_ge(S["psum_zero"], 1)
            pe.wait_ge(S["dve_masks"], 1)
            gram_steps(0, 0, first=True)
            gram_steps(1, 1)
            gram_steps(2, 0)
            with pe.Fori(1, PAIRS // 2 - 1) as q:
                gram_steps(2 * q + 1, 1)
                gram_steps(2 * q + 2, 0)
            gram_steps(PAIRS - 1, 1)
            gram(PAIRS - 1, CHUNKS - 1, (PAIRS - 1 + CHUNKS - 1) % 2, 1)

            def small(ready, count, out, lhsT, rhs, done):
                pe.wait_ge(S[ready], count)
                mm(out, lhsT, rhs, start=True, stop=True).then_inc(S[done], 1)
            small("sums_ready", 1, ps[:, 0, 0:2 * PAIRS], pairm[:], sd[:].rearrange("p a n -> p (a n)"), "gmean_ps")
            small("vec_ready", 3, ps[:, 1, 0:3 * PAIRS * ZG], blockm[:], v3[:].rearrange("p k n e -> p (k n e)"), "vec4_ps")
            small("cov_part", 2, ps[:, 2, 0:1 + ZG], foldm[:], cz[:], "cov_ps")
            small("mu_ready", 1, ps[:, 3, 0:ZG], blockm[:], mu4[:], "mu4_ps")
            pe.wait_ge(S["ns_in"], 2)
            for n in range(NS):
                after(pe, "ns_y", n)
                after(pe, "ns_z", n)
                Y, Z = Yb[:, n % 2, :], Zb[:, n % 2, :]
                mm(ps[:, 0, 0:P], Z, Y, start=True, stop=True).then_inc(S["ns_m"], 1)
                pe.wait_ge(S["ns_t"], n + 1)
                mm(ps[:, 1, 0:P], Y, Tm[:], start=True, stop=True).then_inc(S["ns_y_ps"], 1)
                mm(ps[:, 2, 0:P], Tm[:], Z, start=True, stop=True).then_inc(S["ns_z_ps"], 1)
            pe.wait_ge(S["diagw_ready"], 1)
            small("ns_z", NS, ps[:, 3, 0:P], Zb[:, NS % 2, :], diagw[:], "pw_ps")
            small("pw_ready", 1, ps[:, 4, 0:PAIRS], pw[:], t8[:], "dv_ps")

            def mix(p, b):
                pe.wait_ge(S["amat_ready"], p + 1)
                mm(ps[:, 1, bass.ds(p * (1 + ZG), 1 + ZG)], amat[:, b, :],
                   g5[:, bass.ds(p, 1), :].rearrange("p a e -> p (a e)"), start=True, stop=True).then_inc(S["ag_ps"], 1)
                for c in range(NW):
                    n4 = 4 * p + (c // 2) - 1
                    after(pe, "mix_act" if c % 2 == 0 else "mix_dve", n4)
                    mm(ps[:, 2 + c % 4, 0:392], amat[:, b, :], X[:, p, c * 392:(c + 1) * 392],
                       start=True, stop=True).then_inc(S["mix_ps"], 1)
            pe.wait_ge(S["ns_y"], NS)
            pe.wait_ge(S["d_ready"], 1)
            mix(0, 0)
            with pe.Fori(0, PAIRS // 2 - 1) as q:
                mix(2 * q + 1, 1)
                mix(2 * q + 2, 0)
            mix(PAIRS - 1, 1)
            small("sums2_ready", 1, ps[:, 0, 0:2 * PAIRS], pairm[:], sd[:].rearrange("p a n -> p (a n)"), "gmean2_ps")

            def scores_for_exp(u, par, t):
                after(pe, "prob_ready", TILES * u + t - 1)
                for m in range(2):
                    o = ps[64 * m:64 * m + POS, B_ST[t % 2], 0:ST]
                    mm(o, qk[par][:, m, t // 2, 2 + t % 2, :],
                       diag[par][:, :, m, t // 2, t % 2, :], start=True, stop=False)
                    ins = mm(o, sel[:, m * TILES + t, :], mdiag[par][:].rearrange("p h q -> p (h q)"),
                             start=False, stop=True)
                ins.then_inc(S["st_ps"], 1)

            def scores_for_max(u, par, t):
                after(pe, "max_ready", TILES * u + t - 1)
                for m in range(2):
                    ins = mm(ps[64 * m:64 * m + POS, B_S[t % 2], 0:ST],
                             qk[par][:, m, t // 2, t % 2, :].bitcast(BF16)[:, 1::2],
                             diag[par][:].bitcast(BF16)[:, :, m, t // 2, 2 + t % 2, 1::2], start=True, stop=True)
                ins.then_inc(S["s_ps"], 1)

            def weigh_values(v_, par, t):
                k, ab = t // 2, t % 2
                after(pe, "prob_ready", TILES * v_ + t + 1)
                for j4 in range(2):
                    for jj in range(4):
                        mm(ps[32 * jj:32 * jj + 32, B_O[k], bass.ds((2 * ab + j4) * POS, POS)],
                           vst[par][0:64 + POS, k, 2 * ab + j4, jj].rearrange("p i d -> p (i d)"),
                           prob[par][0:64 + POS, t, 4 * j4 + jj, :], start=True, stop=True)
                for jj in range(4):
                    pv = prob[par][0:64 + POS, t].rearrange("p (a j) q -> p a j q", a=2)[:, :, jj, :]
                    ins = mm(ps[32 * jj:32 * jj + 32, B_O[k], bass.ds(TOK + 2 * ab * POS, 2 * POS)],
                             ones_kd[0:64 + POS, :], pv, start=True, stop=True)
                ins.then_inc(S["pv_ps"], 1)

            def project_values(w, par, lo, hi):
                for n in range(lo, hi):
                    k, a_ = n // SUB, n % SUB
                    for m in range(2):
                        ins = mm(ps[64 * m:64 * m + POS, B_V, n * C:(n + 1) * C],
                                 xn[par][:, k, :].rearrange("p (s a) -> p a s", a=SUB)[:, a_, :], wv[:, m, :],
                                 start=True, stop=True)
                return ins

            def body(i, par):
                u, w, s, z = i, i + 2, i + 1, i - 1
                if has(z):
                    after(pe, "o_ready", KH * z)
                    after(pe, "v_act", z + 1)
                    after(pe, "v_dve", z + 1)
                for t in range(TILES):
                    if has(z):
                        weigh_values(z, 1 - par, t)
                    if has(u):
                        if t == 0:
                            after(pe, "mdiag_ready", u + 1)
                            pe.wait_ge(diag_in[par], 16 * HH * (u // 2 + 1))
                        scores_for_exp(u, par, t)

                def project_qk(m):
                    after(pe, "qk_ready", 2 * w + m)
                    mm(ps[:, B_QK, 0:UT], wqk[:, m, :], xn[par][:].rearrange("p k t -> p (k t)"),
                       start=True, stop=True).then_inc(S["qk_ps"], 1)
                if has(w):
                    after(pe, "xn_ready", KH * (w + 1))
                    project_qk(0)
                    after(pe, "v_act", w)
                    after(pe, "v_dve", w)
                    project_values(w, par, 0, 3)
                    project_qk(1)
                    project_values(w, par, 3, 4)
                if has(s):
                    pe.wait_ge(diag_in[1 - par], 16 * HH * (s // 2 + 1))
                    after(pe, "mdiag_ready", s)
                    scores_for_max(s, 1 - par, 0)
                    scores_for_max(s, 1 - par, 1)
                if has(w):
                    project_values(w, par, 4, 6)
                if has(s):
                    scores_for_max(s, 1 - par, 2)
                    scores_for_max(s, 1 - par, 3)
                if has(w):
                    project_values(w, par, 6, 8).then_inc(S["v_ps"], 1)
                if has(s):
                    after(pe, "max_ready", TILES * (s + 1))
                    for m in range(2):
                        ins = mm(ps[32 * m:32 * m + 32, B_S[0], 448:448 + POS],
                                 rmax[1 - par][0:64 + POS].rearrange("p t h -> p (t h)"),
                                 identb[0:64 + POS, 64 * m:64 * m + POS], start=True, stop=True)
                    ins.then_inc(S["mt_ps"], 1)
            pe.wait_ge(S["const_dma"], 48)
            pe.wait_ge(S["psum_zero"], 2)
            pipeline(pe, body)


def kernel(x, L0_conv_weight, L0_conv_bias, L1_conv_bn_gamma, L1_conv_bn_beta, L1_conv_bn_mean,
           L1_conv_bn_var, L1_conv_qk_w, L1_conv_v_w):
    import concourse.bacc as bacc
    from concourse.bass_utils import run_bass_kernel_spmd

    def rows(a):
        a = np.ascontiguousarray(a).reshape(4, 1, 16, -1)
        return np.broadcast_to(a, (4, 2, 16, a.shape[-1])).reshape(128, a.shape[-1])

    def by_image(w):
        t = np.zeros((4, 2, 16, 2, w.shape[0]), w.dtype)
        for m in range(2):
            t[:, m, :, m] = w.T.reshape(4, 16, -1)
        return t.reshape(128, 2, w.shape[0])

    params = np.concatenate([rows(a) for a in (L0_conv_weight, L0_conv_bias, L1_conv_bn_gamma, L1_conv_bn_beta,
                                               L1_conv_bn_mean, L1_conv_bn_var)], axis=1)
    arrays = {"x_in": np.ascontiguousarray(x), "params": params, "w_qk": by_image(np.asarray(L1_conv_qk_w)),
              "w_v": by_image(np.asarray(L1_conv_v_w))}
    nc = bacc.Bacc("TRN2", target_bir_lowering=False, num_devices=1)
    args = [nc.dram_tensor(n, a.shape, mybir.dt.from_np(a.dtype), kind="ExternalInput").ap()
            for n, a in arrays.items()]
    out = nc.dram_tensor("out", (N, C, H, W), F32, kind="ExternalOutput").ap()
    conv_preact_kernel(nc, *args, out)
    r = run_bass_kernel_spmd(nc, [arrays], core_ids=[0])
    return r.results[0]["out"]
```

```python
from contextlib import ExitStack

import numpy as np
import concourse.bass as bass
from concourse import mybir

F32 = mybir.dt.float32
BF16 = mybir.dt.bfloat16
ALU = mybir.AluOpType
ACT = mybir.ActivationFunctionType
AX = mybir.AxisListType

N, C, H, W = 16, 64, 56, 56
P = 128
PAIRS = N // 2
HW = H * W
WS, NW = 7, H // 7
POS = WS * WS
SUB = 4
TOK = POS * SUB
KH = NW // SUB
UNITS = PAIRS * NW
UT = KH * TOK
HEADS, DH = 16, 16
HH = HEADS // 2
TILES = KH * 2
ST = HH * POS
ZG = 4
SCALE = DH ** -0.5

GN_EPS, BN_EPS, ZCA_EPS = 1e-5, 1e-6, 1e-4
GN_COUNT = 2 * HW
ZCA_COUNT = N * HW

BLK = 112
CB = 4
CHUNK = BLK * CB
CHUNKS = HW // CHUNK


def newton_schulz_scales():
    top = ZG + 2 * ZCA_EPS
    low = (0.5 * ZCA_EPS / top) ** 0.5
    scales = []
    while low < 1 - 1e-3:
        a = (3.0 / (1 + low + low * low)) ** 0.5
        scales.append(a)
        low = a * low * (3 - a * a * low * low) / 2
    return top, scales + [1.0, 1.0]


def conv_preact_kernel(nc, x, params, w_qk, w_v, out):
    top, scales = newton_schulz_scales()
    NS = len(scales)
    x_d = x.rearrange("(p i) (j d) h w -> p j i d (h w)", i=2, j=4)
    out_d = out.rearrange("(p i) (j d) h w -> p j i d (h w)", i=2, j=4)
    BANDS = [(j, i) for j in range(4) for i in range(2)]

    with ExitStack() as ctx:
        def sb(name, shape, dt=F32):
            return ctx.enter_context(nc.sbuf_tensor(name, shape, dt))

        def sem(name):
            return ctx.enter_context(nc.semaphore(name))

        X = sb("X", [P, PAIRS, HW])
        prm = sb("prm", [P, 6])
        wqk = sb("wqk", [P, 2, P])
        wv = sb("wv", [P, 2, C])
        ident = sb("ident", [P, P])
        identb = sb("identb", [P, P], BF16)
        blockm = sb("blockm", [P, P])
        bandm = sb("bandm", [P, 64])
        pairm = sb("pairm", [P, P])
        foldm = sb("foldm", [P, P])
        e4 = sb("e4", [P, ZG])
        headm = sb("headm", [64, HH])
        sel = sb("sel", [P, 8, POS], BF16)
        ones_kd = sb("ones_kd", [P, 32])

        sums = sb("sums", [P, PAIRS])
        g5 = sb("g5", [P, PAIRS, 1 + ZG])
        gmask = sb("gmask", [P, 64])
        t84 = sb("t84", [P, PAIRS, ZG])
        t84b = sb("t84b", [P, PAIRS, ZG])
        c84 = sb("c84", [P, PAIRS, ZG])
        sd = sb("sd", [P, 2, PAIRS])
        mean = sb("mean", [P, PAIRS])
        var = sb("var", [P, PAIRS])
        std = sb("std", [P, PAIRS])
        rinv = sb("rinv", [P, PAIRS])
        usum = sb("usum", [P, PAIRS])
        t8 = sb("t8", [P, PAIRS])
        t8b = sb("t8b", [P, PAIRS])
        v3 = sb("v3", [P, 3, PAIRS, ZG])
        v3n = sb("v3n", [P, 3, PAIRS, ZG])
        cz = sb("cz", [P, 1 + ZG])
        cm = sb("cm", [P, 1 + ZG])
        mu4 = sb("mu4", [P, ZG])
        cov4 = sb("cov4", [P, ZG])
        Yb = sb("Yb", [P, 2, P])
        Zb = sb("Zb", [P, 2, P])
        Tm = sb("Tm", [P, P])
        diagw = sb("diagw", [P, P])
        pw = sb("pw", [P, P])
        p4w = sb("p4w", [P, ZG])
        dvec = sb("dvec", [P, PAIRS])
        a4 = sb("a4", [P, PAIRS, ZG])
        ag = sb("ag", [P, PAIRS, 1 + ZG])
        rg5 = sb("rg5", [P, PAIRS, 1 + ZG])
        rinv2 = sb("rinv2", [P, PAIRS])
        amat = sb("amat", [P, 2, P])
        bninv = sb("bninv", [P, 3])
        xn_scale = sb("xn_scale", [P, PAIRS])
        xn_bias = sb("xn_bias", [P, PAIRS])
        xstage = sb("xstage", [P, 2, CHUNK])
        xT = sb("xT", [BLK, 2, CB, 2, 65])

        xn = [sb(f"xn{b}", [P, KH, TOK]) for b in range(2)]
        qk = [sb(f"qk{b}", [P, 2, KH, SUB, POS]) for b in range(2)]
        diag = [sb(f"diag{b}", [P, HH, 2, KH, SUB, POS]) for b in range(2)]
        rmax = [sb(f"rmax{b}", [P, TILES, HH], BF16) for b in range(2)]
        mdiag = [sb(f"mdiag{b}", [P, HH, POS], BF16) for b in range(2)]
        prob = [sb(f"prob{b}", [P, TILES, HH, POS]) for b in range(2)]
        vst = [sb(f"vst{b}", [P, KH, SUB, 4, 2, DH]) for b in range(2)]
        rden = sb("rden", [P, KH, SUB, POS])
        otok = [sb(f"otok{b}", [P, KH, TOK]) for b in range(2)]

        ps = ctx.enter_context(nc.psum_tensor("ps", [P, 8, 512], F32))
        B_QK, B_V, B_S, B_ST, B_O = 0, 1, (2, 3), (4, 5), (6, 7)

        names = (
            "const_dma pool_chain gram_consts masks_ready zeros_ready dve_masks psum_zero load0 load1 staged transposed "
            "xT_ready gram_chunk gram_part gram_kept dve_chain "
            "sums_ready gmean_ps var_ready std_ready vec_ready vec4_ps cov_part cov_ps mu_ready mu4_ps "
            "ns_in ns_m ns_t ns_y_ps ns_z_ps ns_y ns_z diagw_ready pw_ps pw_ready dv_ps d_ready "
            "amat_ready bnvar_ready mix_ps mix_act ag_ps sums2_ready gmean2_ps var2_ready std2_ready "
            "xn_ready qk_ps qk_ready diag0 diag1 v_ps v_act "
            "s_ps max_ready mt_ps mdiag_ready st_ps prob_ready pv_ps rden_ready o_ready x_ready stored"
        ).split()
        S = {n: sem(n) for n in names}
        load = [S["load0"], S["load1"]]
        diag_in = [S["diag0"], S["diag1"]]
        block = ctx.enter_context(nc.Block())

        def after(eng, name, count):
            if isinstance(count, int) and count <= 0:
                return
            eng.wait_ge(S[name], count)

        def pipeline(eng, body):
            for i in range(-2, 4):
                body(i, i % 2)
            with eng.Fori(0, UNITS // 2 - 3) as q:
                body(2 * q + 4, 0)
                body(2 * q + 5, 1)
            for i in range(UNITS - 2, UNITS + 1):
                body(i, i % 2)

        def has(u):
            return not isinstance(u, int) or 0 <= u < UNITS

        @block.sync
        def _(sp):
            for t, src in ((prm[:], params), (wqk[:], w_qk), (wv[:], w_v)):
                sp.dma_start(t, src).then_inc(S["const_dma"], 16)

            def load_pair(p, b):
                for n, (j, i) in enumerate(BANDS):
                    sp.dma_start(X[16 * n:16 * n + 16, p, :], x_d[p, j, i]).then_inc(load[b], 16)
            for b in range(2):
                load_pair(b, b)
            with sp.Fori(1, PAIRS // 2) as q:
                for b in range(2):
                    sp.wait_ge(load[b], 16 * len(BANDS) * q)
                    load_pair(2 * q + b, b)

            def spread(u, par):
                free, ready = sp.snap(TILES * (u - 1)) if not isinstance(u, int) else TILES * (u - 1), 2 * (u + 1)
                after(sp, "st_ps", free)
                after(sp, "qk_ready", ready)
                for h in range(HH):
                    r = slice(16 * h, 16 * h + 16)
                    sp.dma_start(diag[par][r, h].rearrange("p i k a s -> p (i k a s)"),
                                 qk[par][r].rearrange("p i k a s -> p (i k a s)")).then_inc(diag_in[par], 16)

            def store(p, bands):
                for n in bands:
                    sp.dma_start(out_d[p, BANDS[n][0], BANDS[n][1]], X[16 * n:16 * n + 16, p, :]
                                 ).then_inc(S["stored"], 16)

            sp.wait_ge(S["zeros_ready"], 2)
            for i in range(NW):
                spread(i, i % 2)
            with sp.Fori(1, PAIRS) as p:
                for i in range(NW):
                    spread(p * NW + i, i % 2)
                    if 3 <= i < 7:
                        sp.wait_ge(S["x_ready"], KH * NW * p)
                        store(p - 1, (2 * (i - 3), 2 * (i - 3) + 1))
            sp.wait_ge(S["x_ready"], KH * UNITS)
            store(PAIRS - 1, range(len(BANDS)))
            sp.wait_ge(S["stored"], 16 * len(BANDS) * PAIRS)

        @block.gpsimd
        def _(pool):
            steps = [0]

            def chain(ins):
                steps[0] += 1
                ins.then_inc(S["pool_chain"], 1)
                pool.wait_ge(S["pool_chain"], steps[0])

            g = nc.gpsimd
            chain(g.memset(ident[:], 0.0))
            chain(g.affine_select(out=ident[:], in_=ident[:], compare_op=ALU.not_equal, fill=1.0, base=0,
                                  pattern=[[-1, P]], channel_multiplier=1))
            g.memset(xT[:, :, :, :, 64:65], 1.0).then_inc(S["gram_consts"], 1)
            pool.wait_ge(S["gram_consts"], 1)
            for m, k, value in ((blockm, ZG, 1.0), (pairm, 2, 1.0 / GN_COUNT)):
                chain(g.memset(m[:], value))
                v = m[:].rearrange("p (b e) -> p b e", e=k)
                chain(g.affine_select(out=v, in_=v, compare_op=ALU.is_ge, fill=0.0, base=0,
                                      pattern=[[-k, P // k], [0, k]], channel_multiplier=1))
                chain(g.affine_select(out=v, in_=v, compare_op=ALU.is_ge, fill=0.0, base=k - 1,
                                      pattern=[[k, P // k], [0, k]], channel_multiplier=-1))
            chain(g.memset(ones_kd[:], 0.0))
            chain(g.memset(ones_kd[0:POS, 0:16], 1.0))
            g.memset(ones_kd[64:64 + POS, 16:32], 1.0).then_inc(S["masks_ready"], 1)
            pool.wait_ge(S["masks_ready"], 1)
            for b in range(2):
                chain(g.memset(vst[b][:], 0.0))
                chain(g.memset(diag[b][:], 0.0))
                g.memset(mdiag[b][:], 0.0).then_inc(S["zeros_ready"], 1)
                pool.wait_ge(S["zeros_ready"], b + 1)

            def body(i, par):
                v = i - 1
                if has(v):
                    after(pool, "o_ready", KH * (v + 1))
                    xv = X[:, v // NW, :].rearrange("p (a i c k w) -> p i k a c w", a=WS, i=NW, c=WS, k=KH)
                    for k in range(KH):
                        xp = xv[:, v % NW, k].rearrange("p a c w -> p w a c")
                        g.tensor_tensor(xp, xp, otok[1 - par][:, k, :].rearrange("p (w a c) -> p w a c", w=SUB, a=WS),
                                        ALU.add).then_inc(S["x_ready"], 1)
            pipeline(pool, body)

        @block.scalar
        def _(act):
            a = nc.scalar

            def gram_evacuate(p, c, b):
                n = p * CHUNKS + c
                act.wait_ge(S["transposed"], n + 1)
                after(act, "gram_chunk", n - 1)
                a.activation(xT[:, b, :, :, 0:64].rearrange("q k t c -> q (k t) c"),
                             ps[0:BLK, b, 0:CB * P].rearrange("q (k c) -> q k c", c=64),
                             ACT.Copy).then_inc(S["xT_ready"], 1)

            act.wait_ge(S["gram_consts"], 1)
            for c in range(CHUNKS):
                gram_evacuate(0, c, c % 2)
            with act.Fori(0, PAIRS // 2 - 1) as q:
                p = 2 * q + 1
                for b in range(2):
                    for c in range(CHUNKS):
                        gram_evacuate(p + b, c, (1 + b + c) % 2)
            for c in range(CHUNKS):
                gram_evacuate(PAIRS - 1, c, (PAIRS - 1 + c) % 2)

            act.wait_ge(S["var_ready"], 1)
            a.activation(std[:], var[:], ACT.Sqrt).then_inc(S["std_ready"], 1)
            for n, s in enumerate(scales):
                act.wait_ge(S["ns_y_ps"], n + 1)
                a.activation(Yb[:, (n + 1) % 2, :], ps[:, 1, 0:P], ACT.Copy, scale=1.5 * s).then_inc(S["ns_y"], 1)
            act.wait_ge(S["bnvar_ready"], 1)
            a.activation(bninv[:, 1:2], bninv[:, 0:1], ACT.Sqrt).then_inc(S["std2_ready"], 1)
            def mix(p):
                for c in range(NW):
                    act.wait_ge(S["mix_ps"], p * NW + c + 1)
                    a.activation(X[:, p, c * 392:(c + 1) * 392], ps[:, 2 + c % 4, 0:392], ACT.Identity,
                                 bias=dvec[:, bass.ds(p, 1)]).then_inc(S["mix_act"], 1)
            act.wait_ge(S["d_ready"], 1)
            mix(0)
            act.wait_ge(S["var2_ready"], 1)
            a.activation(std[:], var[:], ACT.Sqrt).then_inc(S["std2_ready"], 1)
            with act.Fori(1, PAIRS) as p:
                mix(p)

            def body(i, par):
                u, v = i, i + 1
                for t in range(TILES):
                    if t == 2 and has(v):
                        after(act, "v_ps", v + 1)
                        after(act, "pv_ps", TILES * (v - 1))
                        for m in range(2):
                            for k in range(KH):
                                a.activation(vst[1 - par][64 * m:64 * m + POS, k, :, :, m, :],
                                             ps[64 * k:64 * k + POS, B_V, :]
                                             .rearrange("p (a i j d) -> p i a j d", a=SUB, i=2, j=4)[:, m],
                                             ACT.Relu).then_inc(S["v_act"], 1)
                    if has(u):
                        after(act, "st_ps", TILES * u + t + 1)
                        after(act, "pv_ps", TILES * (u - 2) + t + 1)
                        a.activation(prob[par][:, t], ps[:, B_ST[t % 2], 0:ST].rearrange("p (h q) -> p h q", h=HH),
                                     ACT.Exp, scale=SCALE).then_inc(S["prob_ready"], 1)
                w = i + 2
                if has(w):
                    for m in range(2):
                        after(act, "qk_ps", 2 * w + m + 1)
                        after(act, "st_ps", TILES * (w - 1))
                        a.activation(qk[par][:, m],
                                     ps[:, B_QK, 0:UT].rearrange("p (k s a) -> p k a s", k=KH, a=SUB),
                                     ACT.Copy).then_inc(S["qk_ready"], 1)
            act.wait_ge(S["zeros_ready"], 2)
            pipeline(act, body)

        @block.vector
        def _(dve):
            v = nc.vector
            steps = [0]

            def chain(ins):
                steps[0] += 1
                ins.then_inc(S["dve_chain"], 1)
                dve.wait_ge(S["dve_chain"], steps[0])

            v.memset(ps[:], 0.0).then_inc(S["psum_zero"], 1)
            def stage(p, c, b):
                n = p * CHUNKS + c
                after(dve, "transposed", n - 1)
                v.tensor_copy(xstage[:, b, :], X[:, p, c * CHUNK:(c + 1) * CHUNK]).then_inc(S["staged"], 1)

            def keep_gram(p, b):
                dve.wait_ge(S["gram_chunk"], CHUNKS * (p + 1))
                after(dve, "gram_kept", p)
                v.tensor_tensor(gmask[:], ps[:, 2 + b, 0:64], bandm[:], ALU.mult).then_inc(S["gram_part"], 1)
                v.tensor_copy(g5[:, bass.ds(p, 1), 0:1], ps[:, 2 + b, 64:65].rearrange("p (a b) -> p a b", a=1)
                              ).then_inc(S["gram_part"], 1)
                dve.wait_ge(S["gram_part"], 2 * (p + 1))
                v.tensor_reduce(g5[:, bass.ds(p, 1), 1:], gmask[:].rearrange("p (o b e) -> p o e b", o=1, e=ZG),
                                AX.X, ALU.add).then_inc(S["gram_kept"], 1)

            def stage_pair(p, b, first=False):
                dve.wait_ge(load[b], 16 * 8 * (p // 2 + 1))
                for c in range(CHUNKS):
                    stage(p, c, (b + c) % 2)
                    if c == 2 and not first:
                        keep_gram(p - 1, 1 - b)
            stage_pair(0, 0, first=True)
            dve.wait_ge(S["masks_ready"], 1)
            v.tensor_copy(identb[:], ident[:])
            v.tensor_reduce(e4[:], ident[:].rearrange("p (b e) -> p e b", e=ZG), AX.X, ALU.add)
            v.tensor_reduce(headm[:], ident[0:64, 0:64].rearrange("p (b e) -> p e b", e=HH), AX.X, ALU.add, negate=True)
            chain(v.tensor_reduce(t8[:], ident[:, 0:64].rearrange("p (g e) -> p g e", e=8), AX.X, ALU.add))
            v.tensor_copy(sel[:], t8[:].rearrange("p (g o) -> p g o", o=1).broadcast_to([P, 8, POS]))
            v.tensor_tensor(bandm[:], blockm[:, 0:64], blockm[:, 64:P], ALU.add)
            iv = ident[:].rearrange("p (j i d) -> p j i d", j=4, i=2)
            fv = foldm[:].rearrange("p (j i d) -> p j i d", j=4, i=2)
            v.tensor_tensor(fv[:, :, 0, :], iv[:, :, 0, :], iv[:, :, 1, :], ALU.add)
            chain(v.tensor_tensor(fv[:, :, 1, :], iv[:, :, 0, :], iv[:, :, 1, :], ALU.add))
            chain(v.tensor_scalar(foldm[:], foldm[:], 1.0 / ZCA_COUNT, None, ALU.mult))
            v.memset(bninv[:], 0.0).then_inc(S["dve_masks"], 1)
            dve.wait_ge(S["dve_masks"], 1)

            stage_pair(1, 1)
            stage_pair(2, 0)
            with dve.Fori(1, PAIRS // 2 - 1) as q:
                stage_pair(2 * q + 1, 1)
                stage_pair(2 * q + 2, 0)
            stage_pair(PAIRS - 1, 1)
            keep_gram(PAIRS - 1, 1)
            dve.wait_ge(S["gram_kept"], PAIRS)

            def over_pairs(ap):
                return ap.rearrange("p (n o) -> p n o", o=1).broadcast_to([P, PAIRS, ZG])

            def over_group(ap):
                return ap.rearrange("p (o e) -> p o e", o=1).broadcast_to([P, PAIRS, ZG])

            def rsqrt(y, x_, s_, t_):
                chain(v.reciprocal(y, s_))
                chain(v.tensor_tensor(t_, y, y, ALU.mult))
                chain(v.tensor_tensor(t_, t_, x_, ALU.mult))
                chain(v.tensor_scalar(t_, t_, -0.5, 1.5, ALU.mult, ALU.add))
                chain(v.tensor_tensor(y, y, t_, ALU.mult))

            chain(v.tensor_tensor(t84[:], g5[:, :, 1:], over_group(e4[:]), ALU.mult))
            v.tensor_copy(sd[:, 0, :], g5[:, :, 0])
            v.tensor_copy(sums[:], g5[:, :, 0])
            chain(v.tensor_reduce(sd[:, 1, :], t84[:], AX.X, ALU.add))
            v.tensor_copy(t8b[:], sums[:]).then_inc(S["sums_ready"], 1)
            dve.wait_ge(S["gmean_ps"], 1)

            def group_var(col):
                chain(v.tensor_copy(mean[:], ps[:, 0, col:col + PAIRS]))
                chain(v.tensor_tensor(t8[:], mean[:], mean[:], ALU.mult))
                return v.scalar_tensor_tensor(var[:], ps[:, 0, col + PAIRS:col + 2 * PAIRS], GN_EPS, t8[:],
                                              ALU.add, ALU.subtract)
            dve.wait_ge(S["sums_ready"], 1)
            group_var(0).then_inc(S["var_ready"], 1)
            dve.wait_ge(S["var_ready"], 1)
            dve.wait_ge(S["std_ready"], 1)
            rsqrt(rinv[:], var[:], std[:], t8[:])
            chain(v.scalar_tensor_tensor(usum[:], mean[:], -float(HW), sums[:], ALU.mult, ALU.add))
            for k, vec in enumerate((rinv, mean, sums)):
                v.tensor_tensor(v3[:, k], over_pairs(vec[:]), over_group(e4[:]), ALU.mult).then_inc(S["vec_ready"], 1)
            dve.wait_ge(S["vec4_ps"], 1)
            chain(v.tensor_copy(v3n[:], ps[:, 1, 0:3 * PAIRS * ZG].rearrange("p (k n e) -> p k n e", k=3, n=PAIRS)))
            chain(v.tensor_tensor(t84[:], v3n[:, 1], over_pairs(usum[:]), ALU.mult))
            chain(v.tensor_tensor(t84b[:], v3n[:, 2], over_pairs(mean[:]), ALU.mult))
            chain(v.tensor_tensor(c84[:], g5[:, :, 1:], t84[:], ALU.subtract))
            chain(v.tensor_tensor(c84[:], c84[:], t84b[:], ALU.subtract))
            chain(v.tensor_tensor(c84[:], c84[:], v3n[:, 0], ALU.mult))
            chain(v.tensor_tensor(c84[:], c84[:], over_pairs(rinv[:]), ALU.mult))
            chain(v.tensor_tensor(t8[:], usum[:], rinv[:], ALU.mult))
            v.tensor_reduce(cz[:, 0:1], t8[:], AX.X, ALU.add).then_inc(S["cov_part"], 1)
            v.tensor_reduce(cz[:, 1:], c84[:].rearrange("p n e -> p e n"), AX.X, ALU.add).then_inc(S["cov_part"], 1)
            dve.wait_ge(S["cov_ps"], 1)
            chain(v.tensor_copy(cm[:], ps[:, 2, 0:1 + ZG]))
            v.tensor_scalar(mu4[:], e4[:], cm[:, 0:1], None, ALU.mult).then_inc(S["mu_ready"], 1)
            dve.wait_ge(S["mu4_ps"], 1)
            chain(v.tensor_scalar(cov4[:], ps[:, 3, 0:ZG], cm[:, 0:1], None, ALU.mult))
            chain(v.tensor_tensor(cov4[:], cm[:, 1:], cov4[:], ALU.subtract))
            chain(v.scalar_tensor_tensor(cov4[:], e4[:], ZCA_EPS, cov4[:], ALU.mult, ALU.add))
            chain(v.tensor_scalar(cov4[:], cov4[:], 1.0 / top, None, ALU.mult))
            v.tensor_copy(Zb[:, 0, :], ident[:]).then_inc(S["ns_in"], 1)
            v.tensor_tensor(Yb[:, 0, :].rearrange("p (b e) -> p b e", e=ZG), blockm[:].rearrange("p (b e) -> p b e", e=ZG),
                            cov4[:].rearrange("p (o e) -> p o e", o=1).broadcast_to([P, P // ZG, ZG]), ALU.mult
                            ).then_inc(S["ns_in"], 1)
            for n, s in enumerate(scales):
                dve.wait_ge(S["ns_m"], n + 1)
                v.scalar_tensor_tensor(Tm[:], ps[:, 0, 0:P], -s * s / 3, ident[:], ALU.mult, ALU.add
                                       ).then_inc(S["ns_t"], 1)
                dve.wait_ge(S["ns_z_ps"], n + 1)
                v.tensor_scalar(Zb[:, (n + 1) % 2, :], ps[:, 2, 0:P], 1.5 * s, None, ALU.mult).then_inc(S["ns_z"], 1)
            Zn = Zb[:, NS % 2, :]
            dve.wait_ge(S["const_dma"], 48)
            v.tensor_scalar(diagw[:], ident[:], prm[:, 0:1], top ** -0.5, ALU.mult, ALU.mult).then_inc(S["diagw_ready"], 1)
            dve.wait_ge(S["ns_z"], NS)
            chain(v.tensor_reduce(p4w[:], Zn.rearrange("p (b e) -> p e b", e=ZG), AX.X, ALU.add))
            chain(v.tensor_scalar(p4w[:], p4w[:], prm[:, 0:1], top ** -0.5, ALU.mult, ALU.mult))
            chain(v.tensor_tensor(t8[:], rinv[:], mean[:], ALU.mult))
            chain(v.tensor_scalar(t8[:], t8[:], cm[:, 0:1], None, ALU.add))
            chain(v.tensor_tensor(a4[:], v3n[:, 0], p4w[:].rearrange("p (o e) -> p o e", o=1).broadcast_to([P, PAIRS, ZG]), ALU.mult))
            chain(v.tensor_tensor(a4[:], a4[:], over_group(e4[:]), ALU.add))
            chain(v.tensor_tensor(rg5[:], g5[:], rinv[:].rearrange("p (n o) -> p n o", o=1).broadcast_to([P, PAIRS, 1 + ZG]), ALU.mult))
            v.tensor_scalar(bninv[:, 0:1], prm[:, 5:6], BN_EPS, None, ALU.add).then_inc(S["bnvar_ready"], 1)
            dve.wait_ge(S["pw_ps"], 1)
            v.tensor_copy(pw[:], ps[:, 3, 0:P]).then_inc(S["pw_ready"], 1)
            dve.wait_ge(S["dv_ps"], 1)
            v.tensor_scalar(dvec[:], ps[:, 4, 0:PAIRS], -1.0, prm[:, 1:2], ALU.mult, ALU.add).then_inc(S["d_ready"], 1)
            dve.wait_ge(S["d_ready"], 1)
            dve.wait_ge(S["pw_ready"], 1)

            def pair_matrix(p, b):
                after(dve, "mix_ps", NW * (p - 1))
                v.scalar_tensor_tensor(amat[:, b, :], pw[:], rinv[:, bass.ds(p, 1)], ident[:], ALU.mult, ALU.add
                                       ).then_inc(S["amat_ready"], 1)

            for b in range(2):
                pair_matrix(b, b)
            dve.wait_ge(S["ag_ps"], 1)
            chain(v.tensor_tensor(ag[:].rearrange("p n e -> p (n e)"), ps[:, 1, 0:PAIRS * (1 + ZG)],
                                  g5[:].rearrange("p n e -> p (n e)"), ALU.add))
            chain(v.tensor_tensor(t84[:], ag[:, :, 1:], a4[:], ALU.mult))
            chain(v.tensor_reduce(t8[:], t84[:], AX.X, ALU.add))
            chain(v.scalar_tensor_tensor(sd[:, 0, :], dvec[:], float(HW), ag[:, :, 0], ALU.mult, ALU.add))
            chain(v.tensor_tensor(t8b[:], sd[:, 0, :], ag[:, :, 0], ALU.add))
            chain(v.tensor_tensor(t8b[:], t8b[:], dvec[:], ALU.mult))
            v.tensor_tensor(sd[:, 1, :], t8[:], t8b[:], ALU.add).then_inc(S["sums2_ready"], 1)
            dve.wait_ge(S["gmean2_ps"], 1)
            dve.wait_ge(S["sums2_ready"], 1)
            group_var(0).then_inc(S["var2_ready"], 1)
            dve.wait_ge(S["var2_ready"], 1)
            dve.wait_ge(S["std2_ready"], 2)
            rsqrt(rinv2[:], var[:], std[:], t8[:])
            rsqrt(bninv[:, 2:3], bninv[:, 0:1], bninv[:, 1:2], t8[:, 0:1])
            chain(v.tensor_tensor(bninv[:, 2:3], bninv[:, 2:3], prm[:, 2:3], ALU.mult))
            chain(v.tensor_scalar(xn_scale[:], rinv2[:], bninv[:, 2:3], None, ALU.mult))
            chain(v.tensor_tensor(t8[:], mean[:], rinv2[:], ALU.mult))
            chain(v.tensor_scalar(t8[:], t8[:], prm[:, 4:5], bninv[:, 2:3], ALU.add, ALU.mult))
            chain(v.tensor_scalar(xn_bias[:], t8[:], -1.0, prm[:, 3:4], ALU.mult, ALU.add))

            for p in range(2, PAIRS):
                pair_matrix(p, p % 2)
            dve.wait_ge(S["mix_ps"], PAIRS * NW)
            dve.wait_ge(S["mix_act"], PAIRS * NW)
            v.memset(ps[:, B_ST[0]:B_ST[1] + 1, :], 0.0).then_inc(S["psum_zero"], 1)
            v.memset(ps[:, B_S[0]:B_S[1] + 1, :], 0.0).then_inc(S["psum_zero"], 1)
            dve.wait_ge(S["psum_zero"], 3)

            def body(i, par):
                u = i + 2
                if has(u):
                    after(dve, "v_ps", u - 1)
                    xv = X[:, u // NW, :].rearrange("p (a i c k w) -> p i k a c w", a=WS, i=NW, c=WS, k=KH)
                    for k in range(KH):
                        v.tensor_scalar(xn[par][:, k, :].rearrange("p (w a c) -> p w a c", w=SUB, a=WS),
                                        xv[:, u % NW, k].rearrange("p a c w -> p w a c"),
                                        xn_scale[:, bass.ds(u // NW, 1)], xn_bias[:, bass.ds(u // NW, 1)],
                                        ALU.mult, ALU.add).then_inc(S["xn_ready"], 1)
                w, z = i + 1, i - 1

                def divide(k):
                    after(dve, "pv_ps", TILES * z + 2 * k + 2)
                    v.reciprocal(rden[:, k].rearrange("p a s -> p (a s)"), ps[:, B_O[k], TOK:2 * TOK]
                                 ).then_inc(S["rden_ready"], 1)
                    dve.wait_ge(S["rden_ready"], KH * z + k + 1)
                    after(dve, "x_ready", KH * (z - 1))
                    v.tensor_tensor(otok[1 - par][:, k].rearrange("p (s a) -> p a s", a=SUB),
                                    ps[:, B_O[k], 0:TOK].rearrange("p (a s) -> p a s", a=SUB),
                                    rden[:, k], ALU.mult).then_inc(S["o_ready"], 1)
                if has(z):
                    divide(0)
                    divide(1)
                if has(w):
                    for t in range(TILES):
                        after(dve, "s_ps", TILES * w + t + 1)
                        after(dve, "mt_ps", w - 1)
                        v.tensor_reduce(rmax[1 - par][:, t, :], ps[:, B_S[t % 2], 0:ST].rearrange("p (h k) -> p h k", h=HH),
                                        AX.X, ALU.max).then_inc(S["max_ready"], 1)
                    after(dve, "mt_ps", w + 1)
                    after(dve, "st_ps", TILES * (w - 1))
                    v.tensor_tensor(mdiag[1 - par][0:64],
                                    ps[0:64, B_S[0], 448:448 + POS].rearrange("p (o q) -> p o q", o=1).broadcast_to([64, HH, POS]),
                                    headm[:].rearrange("p (h o) -> p h o", o=1).broadcast_to([64, HH, POS]),
                                    ALU.mult).then_inc(S["mdiag_ready"], 1)
            dve.wait_ge(S["zeros_ready"], 2)
            pipeline(dve, body)

        @block.tensor
        def _(pe):
            mm = nc.tensor.matmul

            def transposes(p, c, b):
                n = p * CHUNKS + c
                pe.wait_ge(S["staged"], n + 1)
                after(pe, "xT_ready", n - 1)
                for k in range(CB):
                    ins = nc.tensor.transpose(ps[0:BLK, b, k * P:(k + 1) * P], xstage[:, b, k * BLK:(k + 1) * BLK], ident[:])
                ins.then_inc(S["transposed"], 1)

            def gram(p, c, b, pb):
                pe.wait_ge(S["xT_ready"], p * CHUNKS + c + 1)
                if c == 0:
                    after(pe, "gram_kept", p - 1)
                for k in range(CB):
                    for t in range(2):
                        ins = mm(ps[64 * t:64 * t + 64, 2 + pb, 0:65], xT[:, b, k, t, 0:64], xT[:, b, k, t, :],
                                 start=(c == 0 and k == 0), stop=(c == CHUNKS - 1 and k == CB - 1))
                ins.then_inc(S["gram_chunk"], 1)

            def gram_steps(p, pb, first=False):
                for c in range(CHUNKS):
                    b = (pb + c) % 2
                    transposes(p, c, b)
                    if c > 0:
                        gram(p, c - 1, 1 - b, pb)
                    elif not first:
                        gram(p - 1, CHUNKS - 1, 1 - b, 1 - pb)
            pe.wait_ge(S["psum_zero"], 1)
            pe.wait_ge(S["gram_consts"], 1)
            gram_steps(0, 0, first=True)
            gram_steps(1, 1)
            gram_steps(2, 0)
            with pe.Fori(1, PAIRS // 2 - 1) as q:
                gram_steps(2 * q + 1, 1)
                gram_steps(2 * q + 2, 0)
            gram_steps(PAIRS - 1, 1)
            gram(PAIRS - 1, CHUNKS - 1, (PAIRS - 1 + CHUNKS - 1) % 2, 1)

            def small(ready, count, out, lhsT, rhs, done):
                pe.wait_ge(S[ready], count)
                mm(out, lhsT, rhs, start=True, stop=True).then_inc(S[done], 1)
            small("sums_ready", 1, ps[:, 0, 0:2 * PAIRS], pairm[:], sd[:].rearrange("p a n -> p (a n)"), "gmean_ps")
            small("vec_ready", 3, ps[:, 1, 0:3 * PAIRS * ZG], blockm[:], v3[:].rearrange("p k n e -> p (k n e)"), "vec4_ps")
            small("cov_part", 2, ps[:, 2, 0:1 + ZG], foldm[:], cz[:], "cov_ps")
            small("mu_ready", 1, ps[:, 3, 0:ZG], blockm[:], mu4[:], "mu4_ps")
            pe.wait_ge(S["dve_masks"], 1)
            pe.wait_ge(S["ns_in"], 2)
            for n in range(NS):
                after(pe, "ns_y", n)
                after(pe, "ns_z", n)
                Y, Z = Yb[:, n % 2, :], Zb[:, n % 2, :]
                mm(ps[:, 0, 0:P], Z, Y, start=True, stop=True).then_inc(S["ns_m"], 1)
                pe.wait_ge(S["ns_t"], n + 1)
                mm(ps[:, 1, 0:P], Y, Tm[:], start=True, stop=True).then_inc(S["ns_y_ps"], 1)
                mm(ps[:, 2, 0:P], Tm[:], Z, start=True, stop=True).then_inc(S["ns_z_ps"], 1)
            pe.wait_ge(S["diagw_ready"], 1)
            small("ns_z", NS, ps[:, 3, 0:P], Zb[:, NS % 2, :], diagw[:], "pw_ps")
            small("pw_ready", 1, ps[:, 4, 0:PAIRS], pw[:], t8[:], "dv_ps")

            pe.wait_ge(S["ns_y"], NS)
            small("pw_ready", 1, ps[:, 1, 0:PAIRS * (1 + ZG)], pw[:], rg5[:].rearrange("p n e -> p (n e)"), "ag_ps")

            def mix(p, b):
                pe.wait_ge(S["amat_ready"], p + 1)
                for c in range(NW):
                    after(pe, "mix_act", p * NW + c - 3)
                    mm(ps[:, 2 + c % 4, 0:392], amat[:, b, :], X[:, p, c * 392:(c + 1) * 392],
                       start=True, stop=True).then_inc(S["mix_ps"], 1)
            pe.wait_ge(S["ns_z"], NS)
            pe.wait_ge(S["d_ready"], 1)
            mix(0, 0)
            small("sums2_ready", 1, ps[:, 0, 0:2 * PAIRS], pairm[:], sd[:].rearrange("p a n -> p (a n)"), "gmean2_ps")
            with pe.Fori(0, PAIRS // 2 - 1) as q:
                mix(2 * q + 1, 1)
                mix(2 * q + 2, 0)
            mix(PAIRS - 1, 1)

            def scores_for_exp(u, par, t):
                after(pe, "prob_ready", TILES * u + t - 1)
                for m in range(2):
                    o = ps[64 * m:64 * m + POS, B_ST[t % 2], 0:ST]
                    mm(o, qk[par][:, m, t // 2, 2 + t % 2, :],
                       diag[par][:, :, m, t // 2, t % 2, :], start=True, stop=False)
                    ins = mm(o, sel[:, m * TILES + t, :], mdiag[par][:].rearrange("p h q -> p (h q)"),
                             start=False, stop=True)
                ins.then_inc(S["st_ps"], 1)

            def scores_for_max(u, par, t):
                after(pe, "max_ready", TILES * u + t - 1)
                for m in range(2):
                    ins = mm(ps[64 * m:64 * m + POS, B_S[t % 2], 0:ST],
                             qk[par][:, m, t // 2, t % 2, :].bitcast(BF16)[:, 1::2],
                             diag[par][:].bitcast(BF16)[:, :, m, t // 2, 2 + t % 2, 1::2], start=True, stop=True)
                ins.then_inc(S["s_ps"], 1)

            def weigh_values(v_, par, t):
                k, ab = t // 2, t % 2
                after(pe, "prob_ready", TILES * v_ + t + 1)
                for j4 in range(2):
                    for jj in range(4):
                        mm(ps[32 * jj:32 * jj + 32, B_O[k], bass.ds((2 * ab + j4) * POS, POS)],
                           vst[par][0:64 + POS, k, 2 * ab + j4, jj].rearrange("p i d -> p (i d)"),
                           prob[par][0:64 + POS, t, 4 * j4 + jj, :], start=True, stop=True)
                for jj in range(4):
                    pv = prob[par][0:64 + POS, t].rearrange("p (a j) q -> p a j q", a=2)[:, :, jj, :]
                    ins = mm(ps[32 * jj:32 * jj + 32, B_O[k], bass.ds(TOK + 2 * ab * POS, 2 * POS)],
                             ones_kd[0:64 + POS, :], pv, start=True, stop=True)
                ins.then_inc(S["pv_ps"], 1)

            def project_values(par, a_):
                for k in range(KH):
                    ins = mm(ps[64 * k:64 * k + POS, B_V, a_ * P:(a_ + 1) * P],
                             xn[par][:, k, :].rearrange("p (s a) -> p a s", a=SUB)[:, a_, :],
                             wv[:].rearrange("p i c -> p (i c)"), start=True, stop=True)
                return ins

            def body(i, par):
                u, w, s, z = i, i + 2, i + 1, i - 1
                def weigh(t):
                    if has(z):
                        weigh_values(z, 1 - par, t)

                def score(t):
                    if has(u):
                        scores_for_exp(u, par, t)

                def project_qk(m):
                    if has(w):
                        after(pe, "qk_ready", 2 * w + m)
                        mm(ps[:, B_QK, 0:UT], wqk[:, m, :], xn[par][:].rearrange("p k t -> p (k t)"),
                           start=True, stop=True).then_inc(S["qk_ps"], 1)

                def score_max(t):
                    if has(s):
                        scores_for_max(s, 1 - par, t)

                if has(z):
                    after(pe, "v_act", 4 * (z + 1))
                    after(pe, "o_ready", KH * z - 1)
                weigh(0)
                if has(u):
                    after(pe, "max_ready", TILES * (u + 1))
                    for m in range(2):
                        ins = mm(ps[32 * m:32 * m + 32, B_S[0], 448:448 + POS],
                                 rmax[par][0:64 + POS].rearrange("p t h -> p (t h)"),
                                 identb[0:64 + POS, 64 * m:64 * m + POS], start=True, stop=True)
                    ins.then_inc(S["mt_ps"], 1)
                weigh(1)
                if has(z):
                    after(pe, "o_ready", KH * z)
                weigh(2)
                if has(u):
                    after(pe, "mdiag_ready", u + 1)
                score(0)
                weigh(3)
                score(1)
                score(2)
                score(3)
                if has(w):
                    after(pe, "xn_ready", KH * (w + 1))
                project_qk(0)
                if has(s):
                    pe.wait_ge(diag_in[1 - par], 16 * HH * (s // 2 + 1))
                score_max(0)
                if has(w):
                    after(pe, "v_act", 4 * w)
                    project_values(par, 0)
                    project_values(par, 1)
                score_max(1)
                project_qk(1)
                score_max(2)
                score_max(3)
                if has(w):
                    project_values(par, 2)
                    project_values(par, 3).then_inc(S["v_ps"], 1)
            pe.wait_ge(S["const_dma"], 48)
            pe.wait_ge(S["psum_zero"], 3)
            pe.wait_ge(S["zeros_ready"], 2)
            pipeline(pe, body)


def kernel(x, L0_conv_weight, L0_conv_bias, L1_conv_bn_gamma, L1_conv_bn_beta, L1_conv_bn_mean,
           L1_conv_bn_var, L1_conv_qk_w, L1_conv_v_w):
    import concourse.bacc as bacc
    from concourse.bass_utils import run_bass_kernel_spmd

    def rows(a):
        a = np.ascontiguousarray(a).reshape(4, 1, 16, -1)
        return np.broadcast_to(a, (4, 2, 16, a.shape[-1])).reshape(128, a.shape[-1])

    def by_image(w):
        t = np.zeros((4, 2, 16, 2, w.shape[0]), w.dtype)
        for m in range(2):
            t[:, m, :, m] = w.T.reshape(4, 16, -1)
        return t.reshape(128, 2, w.shape[0])

    params = np.concatenate([rows(a) for a in (L0_conv_weight, L0_conv_bias, L1_conv_bn_gamma, L1_conv_bn_beta,
                                               L1_conv_bn_mean, L1_conv_bn_var)], axis=1)
    arrays = {"x_in": np.ascontiguousarray(x), "params": params, "w_qk": by_image(np.asarray(L1_conv_qk_w)),
              "w_v": by_image(np.asarray(L1_conv_v_w))}
    nc = bacc.Bacc("TRN2", target_bir_lowering=False, num_devices=1)
    args = [nc.dram_tensor(n, a.shape, mybir.dt.from_np(a.dtype), kind="ExternalInput").ap()
            for n, a in arrays.items()]
    out = nc.dram_tensor("out", (N, C, H, W), F32, kind="ExternalOutput").ap()
    conv_preact_kernel(nc, *args, out)
    r = run_bass_kernel_spmd(nc, [arrays], core_ids=[0])
    return r.results[0]["out"]
```

```python
from contextlib import ExitStack

import numpy as np
import concourse.bass as bass
from concourse import mybir

F32 = mybir.dt.float32
BF16 = mybir.dt.bfloat16
ALU = mybir.AluOpType
ACT = mybir.ActivationFunctionType
AX = mybir.AxisListType

N, C, H, W = 16, 64, 56, 56
P = 128
PAIRS = N // 2
HW = H * W
WS, NW = 7, H // 7
POS = WS * WS
SUB = 4
TOK = POS * SUB
KH = NW // SUB
UNITS = PAIRS * NW
UT = KH * TOK
HEADS, DH = 16, 16
HH = HEADS // 2
TILES = KH * 2
ST = HH * POS
ZG = 4
SCALE = DH ** -0.5

GN_EPS, BN_EPS, ZCA_EPS = 1e-5, 1e-6, 1e-4
GN_COUNT = 2 * HW
ZCA_COUNT = N * HW

BLK = 128
BLOCKS = -(-HW // BLK)
CHUNKS = -(-BLOCKS // 4)
CHUNK_FROM = [c * (BLOCKS // CHUNKS) + min(c, BLOCKS % CHUNKS) for c in range(CHUNKS + 1)]
CB = CHUNK_FROM[1]


def chunk_blocks(c):
    return [min(BLK, HW - n * BLK) for n in range(CHUNK_FROM[c], CHUNK_FROM[c + 1])]


def newton_schulz_scales():
    top = ZG + 2 * ZCA_EPS
    low = (0.5 * ZCA_EPS / top) ** 0.5
    scales = []
    while low < 1 - 1e-3:
        a = (3.0 / (1 + low + low * low)) ** 0.5
        scales.append(a)
        low = a * low * (3 - a * a * low * low) / 2
    return top, scales + [1.0, 1.0]


def conv_preact_kernel(nc, x, params, w_qk, w_v, out):
    top, scales = newton_schulz_scales()
    NS = len(scales)
    x_d = x.rearrange("(p i) (j d) h w -> p j i d (h w)", i=2, j=4)
    out_d = out.rearrange("(p i) (j d) h w -> p j i d (h w)", i=2, j=4)
    BANDS = [(j, i) for j in range(4) for i in range(2)]

    with ExitStack() as ctx:
        def sb(name, shape, dt=F32):
            return ctx.enter_context(nc.sbuf_tensor(name, shape, dt))

        def sem(name):
            return ctx.enter_context(nc.semaphore(name))

        X = sb("X", [P, PAIRS, HW])
        prm = sb("prm", [P, 6])
        wqk = sb("wqk", [P, 2, P])
        wv = sb("wv", [P, 2, C])
        ident = sb("ident", [P, P])
        identb = sb("identb", [P, P], BF16)
        blockm = sb("blockm", [P, P])
        bandm = sb("bandm", [P, 64])
        pairm = sb("pairm", [P, P])
        foldm = sb("foldm", [P, P])
        e4 = sb("e4", [P, ZG])
        headm = sb("headm", [64, HH])
        sel = sb("sel", [P, 8, POS], BF16)
        ones_kd = sb("ones_kd", [P, 32])

        sums = sb("sums", [P, PAIRS])
        g5 = sb("g5", [P, PAIRS, 1 + ZG])
        gmask = sb("gmask", [P, 64])
        t84 = sb("t84", [P, PAIRS, ZG])
        t84b = sb("t84b", [P, PAIRS, ZG])
        c84 = sb("c84", [P, PAIRS, ZG])
        sd = sb("sd", [P, 2, PAIRS])
        mean = sb("mean", [P, PAIRS])
        var = sb("var", [P, PAIRS])
        std = sb("std", [P, PAIRS])
        rinv = sb("rinv", [P, PAIRS])
        usum = sb("usum", [P, PAIRS])
        t8 = sb("t8", [P, PAIRS])
        t8b = sb("t8b", [P, PAIRS])
        v3 = sb("v3", [P, 3, PAIRS, ZG])
        v3n = sb("v3n", [P, 3, PAIRS, ZG])
        cz = sb("cz", [P, 1 + ZG])
        cm = sb("cm", [P, 1 + ZG])
        rep_in = sb("rep_in", [P, 2 * ZG + ZG * ZG])
        full = sb("full", [P, 2 * ZG + ZG * ZG])
        eye4 = sb("eye4", [P, ZG, ZG])
        yz = sb("yz", [P, 2, 2, ZG, ZG])
        prods = sb("prods", [P, 2, ZG, ZG, ZG])
        ms = sb("ms", [P, ZG, ZG])
        pw = sb("pw", [P, P])
        zcol = sb("zcol", [P, ZG])
        p4w = sb("p4w", [P, ZG])
        dvec = sb("dvec", [P, PAIRS])
        a4 = sb("a4", [P, PAIRS, ZG])
        ag = sb("ag", [P, PAIRS, 1 + ZG])
        rg5 = sb("rg5", [P, PAIRS, 1 + ZG])
        rinv2 = sb("rinv2", [P, PAIRS])
        amat = sb("amat", [P, PAIRS, P])
        bninv = sb("bninv", [P, 3])
        xn_scale = sb("xn_scale", [P, PAIRS])
        xn_bias = sb("xn_bias", [P, PAIRS])
        xstage = sb("xstage", [P, 2, CB * BLK])
        xT = sb("xT", [BLK, 2, CB, 2, 65])

        xn = [sb(f"xn{b}", [P, KH, TOK]) for b in range(2)]
        qk = [sb(f"qk{b}", [P, 2, KH, SUB, POS]) for b in range(2)]
        diag = [sb(f"diag{b}", [P, HH, 2, KH, SUB, POS]) for b in range(2)]
        rmax = [sb(f"rmax{b}", [P, TILES, HH], BF16) for b in range(2)]
        mdiag = [sb(f"mdiag{b}", [P, HH, POS], BF16) for b in range(2)]
        prob = [sb(f"prob{b}", [P, TILES, HH, POS]) for b in range(2)]
        vst = [sb(f"vst{b}", [P, KH, SUB, 4, 2, DH]) for b in range(2)]
        rden = sb("rden", [P, KH, SUB, POS])
        otok = [sb(f"otok{b}", [P, KH, TOK]) for b in range(2)]

        ps = ctx.enter_context(nc.psum_tensor("ps", [P, 8, 512], F32))
        B_QK, B_V, B_S, B_ST, B_O = 0, 1, (2, 3), (4, 5), (6, 7)

        B_MIX = (6, 7, 4, 5)

        names = (
            "const_dma pool_chain gram_consts masks_ready zeros_ready dve_masks psum_zero load0 load1 staged transposed "
            "xT_ready root_near gram_chunk gram_part gram_kept dve_chain "
            "sums_ready gmean_ps var_ready std_ready vec_ready vec4_ps cov_part cov_ps row_ready full_ps "
            "pw_ready dv_ps d_ready "
            "amat_ready bnvar_ready mix_ps mix_act ag_ps sums2_ready gmean2_ps var2_ready std2_ready "
            "xn_ready qk_ps qk_ready diag0 diag1 v_ps v_act "
            "s_ps max_ready mt_ps mdiag_ready st_ps prob_ready pv_ps den_ps rden_ready o_ready x_ready stored"
        ).split()
        S = {n: sem(n) for n in names}
        load = [S["load0"], S["load1"]]
        diag_in = [S["diag0"], S["diag1"]]
        block = ctx.enter_context(nc.Block())

        def after(eng, name, count):
            if isinstance(count, int) and count <= 0:
                return
            eng.wait_ge(S[name], count)

        mixed_after = {-2: range(2, 5), -1: range(5, PAIRS)}

        def pipeline(eng, body, mix=None):
            for i in range(-2, 4):
                body(i, i % 2)
                if mix:
                    for p in mixed_after.get(i, ()):
                        mix(p)
            with eng.Fori(0, UNITS // 2 - 3) as q:
                body(2 * q + 4, 0)
                body(2 * q + 5, 1)
            for i in range(UNITS - 2, UNITS + 1):
                body(i, i % 2)

        def has(u):
            return not isinstance(u, int) or 0 <= u < UNITS

        @block.sync
        def _(sp):
            def load_pair(p, b):
                for n, (j, i) in enumerate(BANDS):
                    sp.dma_start(X[16 * n:16 * n + 16, p, :], x_d[p, j, i]).then_inc(load[b], 16)
            load_pair(0, 0)
            for t, src in ((prm[:], params), (wqk[:], w_qk), (wv[:], w_v)):
                sp.dma_start(t, src).then_inc(S["const_dma"], 16)
            load_pair(1, 1)
            with sp.Fori(1, PAIRS // 2) as q:
                for b in range(2):
                    sp.wait_ge(load[b], 16 * len(BANDS) * q)
                    load_pair(2 * q + b, b)

            def spread(u, par):
                free, ready = sp.snap(TILES * (u - 1)) if not isinstance(u, int) else TILES * (u - 1), 2 * (u + 1)
                after(sp, "st_ps", free)
                after(sp, "qk_ready", ready)
                for h in range(HH):
                    r = slice(16 * h, 16 * h + 16)
                    sp.dma_start(diag[par][r, h].rearrange("p i k a s -> p (i k a s)"),
                                 qk[par][r].rearrange("p i k a s -> p (i k a s)")).then_inc(diag_in[par], 16)

            def store(p, bands):
                for n in bands:
                    sp.dma_start(out_d[p, BANDS[n][0], BANDS[n][1]], X[16 * n:16 * n + 16, p, :]
                                 ).then_inc(S["stored"], 16)

            sp.wait_ge(S["zeros_ready"], 2)
            for i in range(NW):
                spread(i, i % 2)
            with sp.Fori(1, PAIRS) as p:
                for i in range(NW):
                    spread(p * NW + i, i % 2)
                    if 3 <= i < 7:
                        sp.wait_ge(S["x_ready"], KH * NW * p)
                        store(p - 1, (2 * (i - 3), 2 * (i - 3) + 1))
            sp.wait_ge(S["x_ready"], KH * UNITS)
            store(PAIRS - 1, range(len(BANDS)))
            sp.wait_ge(S["stored"], 16 * len(BANDS) * PAIRS)

        @block.gpsimd
        def _(pool):
            steps = [0]

            def chain(ins):
                steps[0] += 1
                ins.then_inc(S["pool_chain"], 1)
                pool.wait_ge(S["pool_chain"], steps[0])

            g = nc.gpsimd
            chain(g.memset(ident[:], 0.0))
            chain(g.affine_select(out=ident[:], in_=ident[:], compare_op=ALU.not_equal, fill=1.0, base=0,
                                  pattern=[[-1, P]], channel_multiplier=1))
            g.memset(xT[:, :, :, :, 64:65], 1.0).then_inc(S["gram_consts"], 1)
            pool.wait_ge(S["gram_consts"], 1)
            for m, k, value in ((blockm, ZG, 1.0), (pairm, 2, 1.0 / GN_COUNT)):
                chain(g.memset(m[:], value))
                v = m[:].rearrange("p (b e) -> p b e", e=k)
                chain(g.affine_select(out=v, in_=v, compare_op=ALU.is_ge, fill=0.0, base=0,
                                      pattern=[[-k, P // k], [0, k]], channel_multiplier=1))
                chain(g.affine_select(out=v, in_=v, compare_op=ALU.is_ge, fill=0.0, base=k - 1,
                                      pattern=[[k, P // k], [0, k]], channel_multiplier=-1))
            chain(g.memset(ones_kd[:], 0.0))
            chain(g.memset(ones_kd[0:POS, 0:16], 1.0))
            g.memset(ones_kd[64:64 + POS, 16:32], 1.0).then_inc(S["masks_ready"], 1)
            pool.wait_ge(S["masks_ready"], 1)
            for b in range(2):
                chain(g.memset(vst[b][:], 0.0))
                chain(g.memset(diag[b][:], 0.0))
                g.memset(mdiag[b][:], 0.0).then_inc(S["zeros_ready"], 1)
                pool.wait_ge(S["zeros_ready"], b + 1)

            def body(i, par):
                v = i - 1
                if has(v):
                    xv = X[:, v // NW, :].rearrange("p (a i c k w) -> p i k a c w", a=WS, i=NW, c=WS, k=KH)
                    for k in range(KH):
                        after(pool, "o_ready", KH * v + k + 1)
                        xp = xv[:, v % NW, k].rearrange("p a c w -> p w a c")
                        g.tensor_tensor(xp, xp, otok[1 - par][:, k, :].rearrange("p (w a c) -> p w a c", w=SUB, a=WS),
                                        ALU.add).then_inc(S["x_ready"], 1)
            pipeline(pool, body)

        @block.scalar
        def _(act):
            a = nc.scalar

            def gram_evacuate(p, c, b):
                n = p * CHUNKS + c
                act.wait_ge(S["transposed"], n + 1)
                after(act, "gram_chunk", n - 1)
                blocks = len(chunk_blocks(c))
                a.activation(xT[:, b, 0:blocks, :, 0:64].rearrange("q k t c -> q (k t) c"),
                             ps[:, b, 0:blocks * P].rearrange("q (k c) -> q k c", c=64),
                             ACT.Copy).then_inc(S["xT_ready"], 1)

            act.wait_ge(S["gram_consts"], 1)
            for c in range(CHUNKS):
                gram_evacuate(0, c, c % 2)
            with act.Fori(0, PAIRS // 2 - 1) as q:
                p = 2 * q + 1
                for b in range(2):
                    for c in range(CHUNKS):
                        gram_evacuate(p + b, c, (1 + b + c) % 2)
            for c in range(CHUNKS):
                gram_evacuate(PAIRS - 1, c, (PAIRS - 1 + c) % 2)

            act.wait_ge(S["var_ready"], 1)
            a.activation(std[:], var[:], ACT.Sqrt).then_inc(S["std_ready"], 1)
            act.wait_ge(S["bnvar_ready"], 1)
            a.activation(bninv[:, 1:2], bninv[:, 0:1], ACT.Sqrt).then_inc(S["std2_ready"], 1)
            def mix(p):
                for c in range(NW):
                    act.wait_ge(S["mix_ps"], p * NW + c + 1)
                    a.activation(X[:, p, c * 392:(c + 1) * 392], ps[:, B_MIX[c % 4], 0:392], ACT.Identity,
                                 bias=dvec[:, p:p + 1]).then_inc(S["mix_act"], 1)
            act.wait_ge(S["d_ready"], 1)
            mix(0)
            act.wait_ge(S["var2_ready"], 1)
            a.activation(std[:], var[:], ACT.Sqrt).then_inc(S["std2_ready"], 1)
            mix(1)

            def body(i, par):
                u, v = i, i + 1
                for t in range(TILES):
                    if t == 0 and has(v):
                        after(act, "v_ps", v + 1)
                        after(act, "pv_ps", TILES * (v - 1))
                        for m in range(2):
                            for k in range(KH):
                                a.activation(vst[1 - par][64 * m:64 * m + POS, k, :, :, m, :],
                                             ps[64 * k:64 * k + POS, B_V, :]
                                             .rearrange("p (a i j d) -> p i a j d", a=SUB, i=2, j=4)[:, m],
                                             ACT.Relu).then_inc(S["v_act"], 1)
                    if has(u):
                        after(act, "st_ps", TILES * u + t + 1)
                        after(act, "den_ps", KH * (u - 2) + t // 2 + 1)
                        a.activation(prob[par][:, t], ps[:, B_ST[t % 2], 0:ST].rearrange("p (h q) -> p h q", h=HH),
                                     ACT.Exp, scale=SCALE).then_inc(S["prob_ready"], 1)
                w = i + 2
                if has(w):
                    for m in range(2):
                        after(act, "qk_ps", 2 * w + m + 1)
                        after(act, "st_ps", TILES * (w - 1))
                        a.activation(qk[par][:, m],
                                     ps[:, B_QK, 0:UT].rearrange("p (k s a) -> p k a s", k=KH, a=SUB),
                                     ACT.Copy).then_inc(S["qk_ready"], 1)
            act.wait_ge(S["zeros_ready"], 2)
            pipeline(act, body, mix)

        @block.vector
        def _(dve):
            v = nc.vector
            steps = [0]

            def chain(ins):
                steps[0] += 1
                ins.then_inc(S["dve_chain"], 1)
                dve.wait_ge(S["dve_chain"], steps[0])

            v.memset(ps[:, B_S[0]:B_ST[1] + 1, :], 0.0).then_inc(S["psum_zero"], 1)
            def stage(p, c, b):
                n = p * CHUNKS + c
                after(dve, "transposed", n - 1)
                n_ = sum(chunk_blocks(c))
                v.tensor_copy(xstage[:, b, 0:n_], X[:, p, CHUNK_FROM[c] * BLK:CHUNK_FROM[c] * BLK + n_]).then_inc(S["staged"], 1)

            def keep_gram(p, b):
                dve.wait_ge(S["gram_chunk"], CHUNKS * (p + 1))
                after(dve, "gram_kept", p)
                v.tensor_tensor(gmask[:], ps[:, 2 + b, 0:64], bandm[:], ALU.mult).then_inc(S["gram_part"], 1)
                v.tensor_copy(g5[:, bass.ds(p, 1), 0:1], ps[:, 2 + b, 64:65].rearrange("p (a b) -> p a b", a=1)
                              ).then_inc(S["gram_part"], 1)
                dve.wait_ge(S["gram_part"], 2 * (p + 1))
                v.tensor_reduce(g5[:, bass.ds(p, 1), 1:], gmask[:].rearrange("p (o b e) -> p o e b", o=1, e=ZG),
                                AX.X, ALU.add).then_inc(S["gram_kept"], 1)

            def stage_pair(p, b, first=False):
                dve.wait_ge(load[b], 16 * 8 * (p // 2 + 1))
                for c in range(CHUNKS):
                    stage(p, c, (b + c) % 2)
                    if c == 2 and not first:
                        keep_gram(p - 1, 1 - b)
            stage_pair(0, 0, first=True)
            dve.wait_ge(S["masks_ready"], 1)
            v.tensor_copy(identb[:], ident[:])
            v.tensor_reduce(e4[:], ident[:].rearrange("p (b e) -> p e b", e=ZG), AX.X, ALU.add)
            v.tensor_reduce(headm[:], ident[0:64, 0:64].rearrange("p (b e) -> p e b", e=HH), AX.X, ALU.add, negate=True)
            chain(v.tensor_reduce(t8[:], ident[:, 0:64].rearrange("p (g e) -> p g e", e=8), AX.X, ALU.add))
            v.tensor_copy(sel[:], t8[:].rearrange("p (g o) -> p g o", o=1).broadcast_to([P, 8, POS]))
            v.tensor_tensor(bandm[:], blockm[:, 0:64], blockm[:, 64:P], ALU.add)
            iv = ident[:].rearrange("p (j i d) -> p j i d", j=4, i=2)
            fv = foldm[:].rearrange("p (j i d) -> p j i d", j=4, i=2)
            v.tensor_tensor(fv[:, :, 0, :], iv[:, :, 0, :], iv[:, :, 1, :], ALU.add)
            chain(v.tensor_tensor(fv[:, :, 1, :], iv[:, :, 0, :], iv[:, :, 1, :], ALU.add))
            chain(v.tensor_scalar(foldm[:], foldm[:], 1.0 / ZCA_COUNT, None, ALU.mult))
            chain(v.memset(eye4[:], 0.0))
            chain(v.memset(eye4[:].rearrange("p i j -> p (i j)")[:, 0::ZG + 1], 1.0))
            v.memset(bninv[:], 0.0).then_inc(S["dve_masks"], 1)
            dve.wait_ge(S["dve_masks"], 1)

            stage_pair(1, 1)
            stage_pair(2, 0)
            with dve.Fori(1, PAIRS // 2 - 1) as q:
                stage_pair(2 * q + 1, 1)
                stage_pair(2 * q + 2, 0)
            stage_pair(PAIRS - 1, 1)
            keep_gram(PAIRS - 1, 1)
            dve.wait_ge(S["gram_kept"], PAIRS)

            def over_pairs(ap):
                return ap.rearrange("p (n o) -> p n o", o=1).broadcast_to([P, PAIRS, ZG])

            def over_group(ap):
                return ap.rearrange("p (o e) -> p o e", o=1).broadcast_to([P, PAIRS, ZG])

            def rsqrt(y, x_, s_, t_):
                chain(v.reciprocal(y, s_))
                chain(v.tensor_tensor(t_, y, y, ALU.mult))
                chain(v.tensor_tensor(t_, t_, x_, ALU.mult))
                chain(v.tensor_scalar(t_, t_, -0.5, 1.5, ALU.mult, ALU.add))
                chain(v.tensor_tensor(y, y, t_, ALU.mult))

            chain(v.tensor_tensor(t84[:], g5[:, :, 1:], over_group(e4[:]), ALU.mult))
            v.tensor_copy(sd[:, 0, :], g5[:, :, 0])
            v.tensor_copy(sums[:], g5[:, :, 0])
            chain(v.tensor_reduce(sd[:, 1, :], t84[:], AX.X, ALU.add))
            v.tensor_copy(t8b[:], sums[:]).then_inc(S["sums_ready"], 1)
            dve.wait_ge(S["gmean_ps"], 1)

            def group_var(col):
                chain(v.tensor_copy(mean[:], ps[:, 0, col:col + PAIRS]))
                chain(v.tensor_tensor(t8[:], mean[:], mean[:], ALU.mult))
                return v.scalar_tensor_tensor(var[:], ps[:, 0, col + PAIRS:col + 2 * PAIRS], GN_EPS, t8[:],
                                              ALU.add, ALU.subtract)
            dve.wait_ge(S["sums_ready"], 1)
            group_var(0).then_inc(S["var_ready"], 1)
            dve.wait_ge(S["var_ready"], 1)
            dve.wait_ge(S["std_ready"], 1)
            rsqrt(rinv[:], var[:], std[:], t8[:])
            chain(v.scalar_tensor_tensor(usum[:], mean[:], -float(HW), sums[:], ALU.mult, ALU.add))
            for k, vec in enumerate((rinv, mean, sums)):
                v.tensor_tensor(v3[:, k], over_pairs(vec[:]), over_group(e4[:]), ALU.mult).then_inc(S["vec_ready"], 1)
            dve.wait_ge(S["vec4_ps"], 1)
            chain(v.tensor_copy(v3n[:], ps[:, 1, 0:3 * PAIRS * ZG].rearrange("p (k n e) -> p k n e", k=3, n=PAIRS)))
            chain(v.tensor_tensor(t84[:], v3n[:, 1], over_pairs(usum[:]), ALU.mult))
            chain(v.tensor_tensor(t84b[:], v3n[:, 2], over_pairs(mean[:]), ALU.mult))
            chain(v.tensor_tensor(c84[:], g5[:, :, 1:], t84[:], ALU.subtract))
            chain(v.tensor_tensor(c84[:], c84[:], t84b[:], ALU.subtract))
            chain(v.tensor_tensor(c84[:], c84[:], v3n[:, 0], ALU.mult))
            chain(v.tensor_tensor(c84[:], c84[:], over_pairs(rinv[:]), ALU.mult))
            chain(v.tensor_tensor(t8[:], usum[:], rinv[:], ALU.mult))
            v.tensor_reduce(cz[:, 0:1], t8[:], AX.X, ALU.add).then_inc(S["cov_part"], 1)
            v.tensor_reduce(cz[:, 1:], c84[:].rearrange("p n e -> p e n"), AX.X, ALU.add).then_inc(S["cov_part"], 1)
            dve.wait_ge(S["cov_ps"], 1)
            chain(v.tensor_copy(cm[:], ps[:, 2, 0:1 + ZG]))
            dve.wait_ge(S["const_dma"], 48)
            v.tensor_scalar(rep_in[:, 0:ZG], e4[:], prm[:, 0:1], None, ALU.mult).then_inc(S["row_ready"], 1)
            v.tensor_scalar(rep_in[:, ZG:2 * ZG], e4[:], cm[:, 0:1], top ** -0.5, ALU.mult, ALU.mult
                            ).then_inc(S["row_ready"], 1)
            v.scalar_tensor_tensor(rep_in[:, 2 * ZG:].rearrange("p (i j) -> p i j", j=ZG),
                                   cm[:, 1:].rearrange("p (o j) -> p o j", o=1).broadcast_to([P, ZG, ZG]), 1.0 / top,
                                   e4[:].rearrange("p (i o) -> p i o", o=1).broadcast_to([P, ZG, ZG]),
                                   ALU.mult, ALU.mult).then_inc(S["row_ready"], 1)
            v.tensor_scalar(bninv[:, 0:1], prm[:, 5:6], BN_EPS, None, ALU.add).then_inc(S["bnvar_ready"], 1)
            chain(v.tensor_tensor(t8[:], rinv[:], mean[:], ALU.mult))
            chain(v.tensor_scalar(t8[:], t8[:], cm[:, 0:1], None, ALU.add))
            chain(v.tensor_tensor(rg5[:], g5[:], rinv[:].rearrange("p (n o) -> p n o", o=1).broadcast_to([P, PAIRS, 1 + ZG]), ALU.mult))
            dve.wait_ge(S["full_ps"], 1)
            chain(v.tensor_copy(full[:], ps[:, 3, 0:2 * ZG + ZG * ZG]))

            def rows(m):
                return m.rearrange("p i (o k) -> p i o k", o=1).broadcast_to([P, ZG, ZG, ZG])

            def cols(m):
                return m.rearrange("p k (o j) -> p o j k", o=1).broadcast_to([P, ZG, ZG, ZG])

            w4, m4, y0 = full[:, 0:ZG], full[:, ZG:2 * ZG], yz[:, 0, 0]
            chain(v.tensor_tensor(ms[:], m4.rearrange("p (i o) -> p i o", o=1).broadcast_to([P, ZG, ZG]),
                                  m4.rearrange("p (o j) -> p o j", o=1).broadcast_to([P, ZG, ZG]), ALU.mult))
            chain(v.tensor_tensor(ms[:], full[:, 2 * ZG:].rearrange("p (i j) -> p i j", j=ZG), ms[:], ALU.subtract))
            v.tensor_copy(yz[:, 0, 1], eye4[:])
            chain(v.scalar_tensor_tensor(y0, eye4[:], ZCA_EPS / top, ms[:], ALU.mult, ALU.add))
            grown = 1.0
            for n, s in enumerate(scales):
                Y, Z = yz[:, n % 2, 0], yz[:, n % 2, 1]
                if n > 0:
                    chain(v.tensor_tensor(prods[:, 0], rows(Z), cols(Y), ALU.mult))
                    chain(v.tensor_reduce(ms[:], prods[:, 0], AX.X, ALU.add))
                t_step = v.scalar_tensor_tensor(ms[:], ms[:] if n > 0 else Y, -s * s / 3 * grown * grown, eye4[:],
                                                ALU.mult, ALU.add)
                if n == NS - 4:
                    t_step.then_inc(S["root_near"], 1)
                    dve.wait_ge(S["root_near"], 1)
                else:
                    chain(t_step)
                v.tensor_tensor(prods[:, 0], rows(Y), cols(ms[:]), ALU.mult)
                chain(v.tensor_tensor(prods[:, 1], rows(ms[:]), cols(Z), ALU.mult))
                chain(v.tensor_reduce(yz[:, (n + 1) % 2].rearrange("p m i j -> p (m i j)"),
                                      prods[:].rearrange("p m i j k -> p (m i j) k"), AX.X, ALU.add))
                grown *= 1.5 * s
            root = grown * top ** -0.5
            Zn = yz[:, NS % 2, 1]
            chain(v.tensor_tensor(ms[:], Zn, e4[:].rearrange("p (o k) -> p o k", o=1).broadcast_to([P, ZG, ZG]), ALU.mult))
            chain(v.tensor_reduce(zcol[:], ms[:], AX.X, ALU.add))
            chain(v.scalar_tensor_tensor(zcol[:], zcol[:], root, w4, ALU.mult, ALU.mult))
            v.tensor_tensor(pw[:].rearrange("p (b e) -> p b e", e=ZG), blockm[:].rearrange("p (b e) -> p b e", e=ZG),
                            zcol[:].rearrange("p (o e) -> p o e", o=1).broadcast_to([P, P // ZG, ZG]), ALU.mult
                            ).then_inc(S["pw_ready"], 1)
            chain(v.tensor_tensor(ms[:], Zn.rearrange("p i j -> p j i"),
                                  e4[:].rearrange("p (o k) -> p o k", o=1).broadcast_to([P, ZG, ZG]), ALU.mult))
            chain(v.tensor_reduce(p4w[:], ms[:], AX.X, ALU.add))
            chain(v.tensor_scalar(p4w[:], p4w[:], prm[:, 0:1], root, ALU.mult, ALU.mult))
            chain(v.tensor_tensor(a4[:], v3n[:, 0], p4w[:].rearrange("p (o e) -> p o e", o=1).broadcast_to([P, PAIRS, ZG]), ALU.mult))
            chain(v.tensor_tensor(a4[:], a4[:], over_group(e4[:]), ALU.add))
            dve.wait_ge(S["dv_ps"], 1)
            v.tensor_scalar(dvec[:], ps[:, 2, 0:PAIRS], -1.0, prm[:, 1:2], ALU.mult, ALU.add).then_inc(S["d_ready"], 1)
            dve.wait_ge(S["d_ready"], 1)
            dve.wait_ge(S["pw_ready"], 1)

            def pair_matrix(p):
                v.scalar_tensor_tensor(amat[:, p, :], pw[:], rinv[:, p:p + 1], ident[:], ALU.mult, ALU.add
                                       ).then_inc(S["amat_ready"], 1)
            pair_matrix(0)

            dve.wait_ge(S["ag_ps"], 1)
            chain(v.tensor_tensor(ag[:].rearrange("p n e -> p (n e)"), ps[:, 1, 0:PAIRS * (1 + ZG)],
                                  g5[:].rearrange("p n e -> p (n e)"), ALU.add))
            chain(v.tensor_tensor(t84[:], ag[:, :, 1:], a4[:], ALU.mult))
            chain(v.tensor_reduce(t8[:], t84[:], AX.X, ALU.add))
            chain(v.scalar_tensor_tensor(sd[:, 0, :], dvec[:], float(HW), ag[:, :, 0], ALU.mult, ALU.add))
            chain(v.tensor_tensor(t8b[:], sd[:, 0, :], ag[:, :, 0], ALU.add))
            chain(v.tensor_tensor(t8b[:], t8b[:], dvec[:], ALU.mult))
            v.tensor_tensor(sd[:, 1, :], t8[:], t8b[:], ALU.add).then_inc(S["sums2_ready"], 1)
            for p in range(1, PAIRS):
                pair_matrix(p)
            dve.wait_ge(S["gmean2_ps"], 1)
            dve.wait_ge(S["sums2_ready"], 1)
            group_var(0).then_inc(S["var2_ready"], 1)
            dve.wait_ge(S["var2_ready"], 1)
            dve.wait_ge(S["std2_ready"], 2)
            rsqrt(rinv2[:], var[:], std[:], t8[:])
            rsqrt(bninv[:, 2:3], bninv[:, 0:1], bninv[:, 1:2], t8[:, 0:1])
            chain(v.tensor_tensor(bninv[:, 2:3], bninv[:, 2:3], prm[:, 2:3], ALU.mult))
            chain(v.tensor_scalar(xn_scale[:], rinv2[:], bninv[:, 2:3], None, ALU.mult))
            chain(v.tensor_tensor(t8[:], mean[:], rinv2[:], ALU.mult))
            chain(v.tensor_scalar(t8[:], t8[:], prm[:, 4:5], bninv[:, 2:3], ALU.add, ALU.mult))
            chain(v.tensor_scalar(xn_bias[:], t8[:], -1.0, prm[:, 3:4], ALU.mult, ALU.add))

            dve.wait_ge(S["mix_act"], NW)

            def body(i, par):
                u = i + 2
                if isinstance(i, int) and i == 3:
                    dve.wait_ge(S["mix_act"], PAIRS * NW)
                if has(u):
                    after(dve, "v_ps", u - 1)
                    xv = X[:, u // NW, :].rearrange("p (a i c k w) -> p i k a c w", a=WS, i=NW, c=WS, k=KH)
                    for k in range(KH):
                        v.tensor_scalar(xn[par][:, k, :].rearrange("p (w a c) -> p w a c", w=SUB, a=WS),
                                        xv[:, u % NW, k].rearrange("p a c w -> p w a c"),
                                        xn_scale[:, bass.ds(u // NW, 1)], xn_bias[:, bass.ds(u // NW, 1)],
                                        ALU.mult, ALU.add).then_inc(S["xn_ready"], 1)
                w, z = i + 1, i - 1

                def divide(k):
                    after(dve, "den_ps", KH * z + k + 1)
                    v.reciprocal(rden[:, k].rearrange("p a s -> p (a s)"), ps[:, B_O[k], TOK:2 * TOK]
                                 ).then_inc(S["rden_ready"], 1)
                    dve.wait_ge(S["rden_ready"], KH * z + k + 1)
                    after(dve, "x_ready", KH * (z - 1))
                    v.tensor_tensor(otok[1 - par][:, k].rearrange("p (s a) -> p a s", a=SUB),
                                    ps[:, B_O[k], 0:TOK].rearrange("p (a s) -> p a s", a=SUB),
                                    rden[:, k], ALU.mult).then_inc(S["o_ready"], 1)
                if has(z):
                    divide(0)
                    divide(1)
                if has(w):
                    for t in range(TILES):
                        after(dve, "s_ps", TILES * w + t + 1)
                        after(dve, "mt_ps", w - 1)
                        v.tensor_reduce(rmax[1 - par][:, t, :], ps[:, B_S[t % 2], 0:ST].rearrange("p (h k) -> p h k", h=HH),
                                        AX.X, ALU.max).then_inc(S["max_ready"], 1)
                    after(dve, "mt_ps", w + 1)
                    after(dve, "st_ps", TILES * (w - 1))
                    v.tensor_tensor(mdiag[1 - par][0:64],
                                    ps[0:64, B_S[0], 448:448 + POS].rearrange("p (o q) -> p o q", o=1).broadcast_to([64, HH, POS]),
                                    headm[:].rearrange("p (h o) -> p h o", o=1).broadcast_to([64, HH, POS]),
                                    ALU.mult).then_inc(S["mdiag_ready"], 1)
            dve.wait_ge(S["zeros_ready"], 2)
            pipeline(dve, body)

        @block.tensor
        def _(pe):
            mm = nc.tensor.matmul

            def transposes(p, c, b):
                n = p * CHUNKS + c
                pe.wait_ge(S["staged"], n + 1)
                after(pe, "xT_ready", n - 1)
                for k, n_ in enumerate(chunk_blocks(c)):
                    ins = nc.tensor.transpose(ps[0:n_, b, k * P:(k + 1) * P], xstage[:, b, k * BLK:k * BLK + n_], ident[:])
                ins.then_inc(S["transposed"], 1)

            def gram(p, c, b, pb):
                pe.wait_ge(S["xT_ready"], p * CHUNKS + c + 1)
                if c == 0:
                    after(pe, "gram_kept", p - 1)
                blocks = chunk_blocks(c)
                for k, n_ in enumerate(blocks):
                    for t in range(2):
                        ins = mm(ps[64 * t:64 * t + 64, 2 + pb, 0:65], xT[0:n_, b, k, t, 0:64], xT[0:n_, b, k, t, :],
                                 start=(c == 0 and k == 0), stop=(c == CHUNKS - 1 and k == len(blocks) - 1))
                ins.then_inc(S["gram_chunk"], 1)

            def gram_steps(p, pb, first=False):
                for c in range(CHUNKS):
                    b = (pb + c) % 2
                    transposes(p, c, b)
                    if c > 0:
                        gram(p, c - 1, 1 - b, pb)
                    elif not first:
                        gram(p - 1, CHUNKS - 1, 1 - b, 1 - pb)
            def warm_up(count):
                with pe.Fori(0, count // 2):
                    for _ in range(2):
                        mm(ps[:, 7, 0:P], ident[:], ident[:], start=True, stop=True)
            pe.wait_ge(S["gram_consts"], 1)
            warm_up(20)
            pe.wait_ge(S["psum_zero"], 1)
            gram_steps(0, 0, first=True)
            gram_steps(1, 1)
            gram_steps(2, 0)
            with pe.Fori(1, PAIRS // 2 - 1) as q:
                gram_steps(2 * q + 1, 1)
                gram_steps(2 * q + 2, 0)
            gram_steps(PAIRS - 1, 1)
            gram(PAIRS - 1, CHUNKS - 1, (PAIRS - 1 + CHUNKS - 1) % 2, 1)

            def small(ready, count, out, lhsT, rhs, done):
                pe.wait_ge(S[ready], count)
                mm(out, lhsT, rhs, start=True, stop=True).then_inc(S[done], 1)
            small("sums_ready", 1, ps[:, 0, 0:2 * PAIRS], pairm[:], sd[:].rearrange("p a n -> p (a n)"), "gmean_ps")
            small("vec_ready", 3, ps[:, 1, 0:3 * PAIRS * ZG], blockm[:], v3[:].rearrange("p k n e -> p (k n e)"), "vec4_ps")
            small("cov_part", 2, ps[:, 2, 0:1 + ZG], foldm[:], cz[:], "cov_ps")
            small("row_ready", 3, ps[:, 3, 0:2 * ZG + ZG * ZG], blockm[:], rep_in[:], "full_ps")
            pe.wait_ge(S["root_near"], 1)
            warm_up(14)
            small("pw_ready", 1, ps[:, 2, 0:PAIRS], pw[:], t8[:], "dv_ps")

            small("pw_ready", 1, ps[:, 1, 0:PAIRS * (1 + ZG)], pw[:], rg5[:].rearrange("p n e -> p (n e)"), "ag_ps")

            def mix_chunk(p, c, n):
                after(pe, "mix_act", n - 3)
                mm(ps[:, B_MIX[c % 4], 0:392], amat[:, p, :], X[:, p, bass.ds(392 * (n - p * NW), 392)],
                   start=True, stop=True).then_inc(S["mix_ps"], 1)

            def mix(p):
                pe.wait_ge(S["amat_ready"], p + 1)
                with pe.Fori(0, NW // 4) as q:
                    for c in range(4):
                        mix_chunk(p, c, p * NW + 4 * q + c)
            pe.wait_ge(S["amat_ready"], 1)
            for c in range(NW):
                if c == NW // 2:
                    small("sums2_ready", 1, ps[:, 0, 0:2 * PAIRS], pairm[:], sd[:].rearrange("p a n -> p (a n)"), "gmean2_ps")
                mix_chunk(0, c, c)
            mix(1)

            def scores_for_exp(u, par, t):
                after(pe, "prob_ready", TILES * u + t - 1)
                for m in range(2):
                    o = ps[64 * m:64 * m + POS, B_ST[t % 2], 0:ST]
                    mm(o, qk[par][:, m, t // 2, 2 + t % 2, :],
                       diag[par][:, :, m, t // 2, t % 2, :], start=True, stop=False)
                    ins = mm(o, sel[:, m * TILES + t, :], mdiag[par][:].rearrange("p h q -> p (h q)"),
                             start=False, stop=True)
                ins.then_inc(S["st_ps"], 1)

            def scores_for_max(u, par, t):
                after(pe, "max_ready", TILES * u + t - 1)
                for m in range(2):
                    ins = mm(ps[64 * m:64 * m + POS, B_S[t % 2], 0:ST],
                             qk[par][:, m, t // 2, t % 2, :].bitcast(BF16)[:, 1::2],
                             diag[par][:].bitcast(BF16)[:, :, m, t // 2, 2 + t % 2, 1::2], start=True, stop=True)
                ins.then_inc(S["s_ps"], 1)

            def weigh_values(v_, par, t):
                k, ab = t // 2, t % 2
                after(pe, "prob_ready", TILES * v_ + t + 1)
                for j4 in range(2):
                    for jj in range(4):
                        ins = mm(ps[32 * jj:32 * jj + 32, B_O[k], bass.ds((2 * ab + j4) * POS, POS)],
                                 vst[par][0:64 + POS, k, 2 * ab + j4, jj].rearrange("p i d -> p (i d)"),
                                 prob[par][0:64 + POS, t, 4 * j4 + jj, :], start=True, stop=True)
                ins.then_inc(S["pv_ps"], 1)

            def sum_probs(par, k):
                for jj in range(4):
                    pv = prob[par][0:64 + POS, 2 * k:2 * k + 2].rearrange("p t (a j) q -> p (t a) j q", a=2)[:, :, jj, :]
                    ins = mm(ps[32 * jj:32 * jj + 32, B_O[k], TOK:2 * TOK],
                             ones_kd[0:64 + POS, :], pv, start=True, stop=True)
                ins.then_inc(S["den_ps"], 1)

            def project_values(par, a_):
                for k in range(KH):
                    ins = mm(ps[64 * k:64 * k + POS, B_V, a_ * P:(a_ + 1) * P],
                             xn[par][:, k, :].rearrange("p (s a) -> p a s", a=SUB)[:, a_, :],
                             wv[:].rearrange("p i c -> p (i c)"), start=True, stop=True)
                return ins

            def body(i, par):
                u, w, s, z = i, i + 2, i + 1, i - 1

                def weigh(t):
                    if has(z):
                        weigh_values(z, 1 - par, t)

                def denominators(k):
                    if has(z):
                        sum_probs(1 - par, k)

                def score(t):
                    if has(u):
                        scores_for_exp(u, par, t)

                def project_qk(m):
                    if has(w):
                        after(pe, "qk_ready", 2 * w + m)
                        mm(ps[:, B_QK, 0:UT], wqk[:, m, :], xn[par][:].rearrange("p k t -> p (k t)"),
                           start=True, stop=True).then_inc(S["qk_ps"], 1)

                def values(a_):
                    if has(w):
                        if a_ == 0:
                            after(pe, "v_act", 4 * w)
                        ins = project_values(par, a_)
                        if a_ == SUB - 1:
                            ins.then_inc(S["v_ps"], 1)

                def score_max(t):
                    if has(s):
                        scores_for_max(s, 1 - par, t)

                if has(z):
                    after(pe, "v_act", 4 * (z + 1))
                    after(pe, "o_ready", KH * z - 1)
                weigh(0)
                weigh(1)
                denominators(0)
                if has(u):
                    after(pe, "max_ready", TILES * (u + 1))
                    for m in range(2):
                        ins = mm(ps[32 * m:32 * m + 32, B_S[0], 448:448 + POS],
                                 rmax[par][0:64 + POS].rearrange("p t h -> p (t h)"),
                                 identb[0:64 + POS, 64 * m:64 * m + POS], start=True, stop=True)
                    ins.then_inc(S["mt_ps"], 1)
                if has(z):
                    after(pe, "o_ready", KH * z)
                weigh(2)
                weigh(3)
                denominators(1)
                if has(u):
                    after(pe, "mdiag_ready", u + 1)
                if isinstance(i, int) and i == 0:
                    pe.wait_ge(S["mix_act"], PAIRS * NW)
                    zeros = mdiag[1][64:P].rearrange("p h q -> p (h q)")
                    for b in B_ST:
                        mm(ps[:, b, 0:ST], zeros[:, 0:P], zeros, start=True, stop=True)
                for t in range(TILES):
                    score(t)
                if has(w):
                    after(pe, "xn_ready", KH * (w + 1))
                project_qk(0)
                values(0)
                values(1)
                if has(s):
                    pe.wait_ge(diag_in[1 - par], 16 * HH * (s // 2 + 1))
                score_max(0)
                score_max(1)
                project_qk(1)
                score_max(2)
                values(2)
                score_max(3)
                values(3)
            pe.wait_ge(S["const_dma"], 48)
            pe.wait_ge(S["zeros_ready"], 2)
            pipeline(pe, body, mix)


def kernel(x, L0_conv_weight, L0_conv_bias, L1_conv_bn_gamma, L1_conv_bn_beta, L1_conv_bn_mean,
           L1_conv_bn_var, L1_conv_qk_w, L1_conv_v_w):
    import concourse.bacc as bacc
    from concourse.bass_utils import run_bass_kernel_spmd

    def rows(a):
        a = np.ascontiguousarray(a).reshape(4, 1, 16, -1)
        return np.broadcast_to(a, (4, 2, 16, a.shape[-1])).reshape(128, a.shape[-1])

    def by_image(w):
        t = np.zeros((4, 2, 16, 2, w.shape[0]), w.dtype)
        for m in range(2):
            t[:, m, :, m] = w.T.reshape(4, 16, -1)
        return t.reshape(128, 2, w.shape[0])

    params = np.concatenate([rows(a) for a in (L0_conv_weight, L0_conv_bias, L1_conv_bn_gamma, L1_conv_bn_beta,
                                               L1_conv_bn_mean, L1_conv_bn_var)], axis=1)
    arrays = {"x_in": np.ascontiguousarray(x), "params": params, "w_qk": by_image(np.asarray(L1_conv_qk_w)),
              "w_v": by_image(np.asarray(L1_conv_v_w))}
    nc = bacc.Bacc("TRN2", target_bir_lowering=False, num_devices=1)
    args = [nc.dram_tensor(n, a.shape, mybir.dt.from_np(a.dtype), kind="ExternalInput").ap()
            for n, a in arrays.items()]
    out = nc.dram_tensor("out", (N, C, H, W), F32, kind="ExternalOutput").ap()
    conv_preact_kernel(nc, *args, out)
    r = run_bass_kernel_spmd(nc, [arrays], core_ids=[0])
    return r.results[0]["out"]
```
